# Optimizing a Trainium2 kernel written in Bass

```python
import numpy as np
import jax
import jax.numpy as jnp

def _softmax(x, axis=-1):
    return jax.nn.softmax(x, axis=axis)

def _gelu(x):
    return jax.nn.gelu(x, approximate=True)

def _silu(x):
    return jax.nn.silu(x)

def _sigmoid(x):
    return jax.nn.sigmoid(x)

def _layernorm(x, axis=-1, eps=1e-05):
    m = jnp.mean(x, axis=axis, keepdims=True)
    v = jnp.var(x, axis=axis, keepdims=True)
    return (x - m) / jnp.sqrt(v + eps)

def _scatter_add(tgt, idx, src, axis=0):
    return tgt.at[idx].add(src)

def _segment_sum(src, seg, n):
    return jax.ops.segment_sum(src, seg, n)
kernel_name = 'mk_gnn_preln_d1_gnn_r64_351d08'

def setup_inputs(seed: int=0):
    np.random.seed(seed)
    _w = jnp.asarray

    def _rec_inputs():
        import jax
        import jax.numpy as jnp
        _gk = jax.random.key(seed)
        x = -0.0001006 + 1 * jax.random.normal(jax.random.fold_in(_gk, 1), (100000, 96), jnp.float32)
        src = jax.random.randint(jax.random.fold_in(_gk, 2), (25000,), 0, 100000, jnp.int32)
        dst = jax.random.randint(jax.random.fold_in(_gk, 3), (25000,), 0, 100000, jnp.int32)
        _o = jnp.argsort(dst, stable=True)
        src = src[_o]
        dst = dst[_o]
        edge_attr_64 = 0.000189758 + 1.00013 * jax.random.normal(jax.random.fold_in(_gk, 11), (25000, 64), jnp.float32)
        return (x, src, dst, edge_attr_64)
    x, src, dst, edge_attr_64 = _rec_inputs()

    def _L0_gnn_setup():
        import jax, jax.numpy as jnp
        import numpy as np
        N, E = (50000, 12500)
        NODE_DIM, EDGE_DIM = (96, 64)
        IN_DIM = 2 * NODE_DIM + EDGE_DIM
        key = jax.random.key(seed)
        k = jax.random.split(key, 7)
        h = jax.random.normal(k[0], (N, NODE_DIM), dtype=jnp.float32)
        edge_index = jax.random.randint(k[1], (2, E), 0, N, dtype=jnp.int64)
        edge_attr = jax.random.normal(k[2], (E, EDGE_DIM), dtype=jnp.float32)
        s = 1.0 / np.sqrt(IN_DIM)
        W_e = jax.random.uniform(k[3], (IN_DIM, NODE_DIM), jnp.float32, -s, s)
        b_e = jax.random.uniform(k[4], (NODE_DIM,), jnp.float32, -s, s)
        W_n = jax.random.uniform(k[5], (IN_DIM, NODE_DIM), jnp.float32, -s, s)
        b_n = jax.random.uniform(k[6], (NODE_DIM,), jnp.float32, -s, s)
        return {'h': h, 'edge_index': edge_index, 'edge_attr': edge_attr, 'W_e': W_e, 'b_e': b_e, 'W_n': W_n, 'b_n': b_n}
    _L0_gnn_all = _L0_gnn_setup()
    _L0_gnn_in = {k: v for k, v in _L0_gnn_all.items() if k in ('W_e', 'b_e', 'W_n', 'b_n')}
    del _L0_gnn_all
    return {'x': x, 'src': src, 'dst': dst, 'edge_attr_64': edge_attr_64, 'L0_gnn_W_e': _L0_gnn_in['W_e'], 'L0_gnn_b_e': _L0_gnn_in['b_e'], 'L0_gnn_W_n': _L0_gnn_in['W_n'], 'L0_gnn_b_n': _L0_gnn_in['b_n']}

def reference(x, src, dst, edge_attr_64, L0_gnn_W_e, L0_gnn_b_e, L0_gnn_W_n, L0_gnn_b_n):
    import jax
    import jax.numpy as jnp

    def _L0_gnn_ref(h, edge_index, edge_attr, W_e, b_e, W_n, b_n):
        import jax, jax.numpy as jnp
        import numpy as np
        N, E = (50000, 12500)
        NODE_DIM, EDGE_DIM = (96, 64)
        IN_DIM = 2 * NODE_DIM + EDGE_DIM
        src, dst = (edge_index[0], edge_index[1])
        concat = jnp.concatenate([h[src], h[dst], edge_attr], axis=-1)
        gates = jax.nn.sigmoid(concat @ W_e + b_e)
        messages = jax.nn.softplus(concat @ W_n + b_n)
        gated = gates * messages
        n = h.shape[0]
        h_new = jax.ops.segment_sum(gated, dst, num_segments=n)
        edge_count = jax.ops.segment_sum(jnp.ones((dst.shape[0],), h.dtype), dst, num_segments=n)
        edge_count = jnp.clip(edge_count, 1.0, None)[:, None]
        return h + h_new / edge_count
    edge_index = jnp.stack([src, dst])
    h = jnp.maximum(_layernorm(x, axis=-1), 0.0)
    x = x + _L0_gnn_ref(h, edge_index, edge_attr_64, L0_gnn_W_e, L0_gnn_b_e, L0_gnn_W_n, L0_gnn_b_n)
    return x

_drawn_inputs = setup_inputs


def setup_inputs(seed=0):
    import zlib

    import numpy as np

    out = dict(_drawn_inputs(seed))
    spreads = {}
    factors = {'L0_gnn_b_e': 28.764, 'L0_gnn_b_n': 21.866}
    for name, (base, spread) in spreads.items():
        noise = np.random.default_rng([zlib.crc32(name.encode()), seed]).standard_normal(out[name].shape)
        drawn = base * np.exp(spread * noise) if base else spread * noise
        out[name] = jnp.asarray(drawn.astype(out[name].dtype))
    for name, factor in factors.items():
        out[name] = (out[name] * factor).astype(out[name].dtype)
    return out
```

```python
import concourse.bass as bass
from concourse import mybir
from contextlib import ExitStack

FP32 = mybir.dt.float32
I32 = mybir.dt.int32
ALU = mybir.AluOpType
ACT = mybir.ActivationFunctionType
AX = mybir.AxisListType

P = 128
NODES, D = 100000, 96
EDGES, DE = 25000, 64
IN = 2 * D + DE
TILES = -(-EDGES // P)
TB = 4
STEPS = TILES // TB
LAST_EDGES = EDGES - (TILES - 1) * P
R = 16
CHUNK = P * R
ROWS = 2 * TB + R
NS = 3
OUTER = (STEPS - 1) // NS
PAD = float(1 << 20)
AHEAD = 2
EPS = 1e-5
SLACK = AHEAD * CHUNK - (TB - 1) * (CHUNK // TB)
assert STEPS * TB == TILES and OUTER * NS + 1 == STEPS and STEPS * CHUNK >= NODES > (STEPS - 1) * CHUNK


def build(nc, x, src, dst, edge_attr, w_e, b_e, w_n, b_n, out, count_table):
    ctx = ExitStack()
    with ctx:
        def sb(name, shape, dt=FP32):
            return ctx.enter_context(nc.sbuf_tensor(name, shape, dt))

        def pb(name, shape):
            return ctx.enter_context(nc.psum_tensor(name, shape, FP32))

        def sem(name):
            return ctx.enter_context(nc.semaphore(name))

        def sems(name):
            return [sem(f"{name}{u}") for u in range(NS)]

        ident = sb("ident", [P, P])
        ones = sb("ones", [P, P])
        later = sb("later", [P, P])
        weights = sb("weights", [P, 2, 2 * D])
        bias = sb("bias", [1, 2 * D])
        index_rows = sb("index_rows", [P, 3, 2, P], I32)
        index_rows_f = sb("index_rows_f", [P, 3, 2, P])
        limit_i = sb("limit_i", [P, 2], I32)
        limit = sb("limit", [P, 2])
        real = sb("real", [P, 2, P])
        broken = sb("broken", [P, 2, P])
        ahead = sb("ahead", [P, 2, P])
        runs = sb("runs", [P, 2])
        broken_sum = sb("broken_sum", [P, 1])
        runs_sum = sb("runs_sum", [P, 1])
        violations = sb("violations", [P, 1])
        skip = sb("skip", [P, 1])
        flag = sb("flag", [P, 1], I32)
        dst_col = sb("dst_col", [P, 1 + TILES])
        next_col = sb("next_col", [P, TILES])
        gather_f = sb("gather_f", [P, TILES + (NS - 1) * TB, 2])
        scatter_f = sb("scatter_f", [P, TILES])
        gather_idx = [sb(f"gather_idx{u}", [P, TB, 2], I32) for u in range(NS)]
        scatter_idx = [sb(f"scatter_idx{u}", [P, TB], I32) for u in range(NS)]
        node_x = [sb(f"node_x{u}", [P, R, D]) for u in range(NS)]
        node_out = [sb(f"node_out{u}", [P, R, D]) for u in range(NS)]
        edge_x = [sb(f"edge_x{u}", [P, TB, 2, D]) for u in range(NS)]
        concat = [sb(f"concat{u}", [P, TB, IN]) for u in range(NS)]
        dst_across = [sb(f"dst_across{u}", [P, TB, P], I32) for u in range(NS)]
        base = [sb(f"base{u}", [P, TB, D]) for u in range(NS)]
        final = [sb(f"final{u}", [P, TB, D]) for u in range(NS)]
        rstd = [sb(f"rstd{u}", [P, ROWS]) for u in range(NS)]
        shift = [sb(f"shift{u}", [P, ROWS]) for u in range(NS)]
        stats = sb("stats", [P, ROWS, 6])
        half_diff = sb("half_diff", [P, ROWS])
        mean2 = [sb(f"mean2_{u}", [P, ROWS]) for u in range(NS)]
        sq_sum = sb("sq_sum", [P, ROWS])
        diff_sq = sb("diff_sq", [P, ROWS])
        var96 = sb("var96", [P, ROWS])
        log_var = sb("log_var", [P, ROWS])
        rough = sb("rough", [P, ROWS])
        rough_sq = sb("rough_sq", [P, ROWS])
        correction = sb("correction", [P, ROWS])
        concat_t = sb("concat_t", [P, 2, 2, 2, P])
        relu_n = sb("relu_n", [P, TB, D])
        exp_both = sb("exp_both", [P, TB, 2 * D])
        log_n = sb("log_n", [P, TB, D])
        gate_den = sb("gate_den", [P, TB, D])
        gate = sb("gate", [P, TB, D])
        softplus = sb("softplus", [P, TB, D])
        same = sb("same", [P, 2, TB, P])
        count = sb("count", [P, TB])
        inv_count = sb("inv_count", [P, TB])
        messages = sb("messages", [P, TILES, D + 1])
        zeros = sb("zeros", [80, NODES // 80])
        diag = sb("diag", [P, P])
        r_same = sb("r_same", [P, P])
        r_later = sb("r_later", [P, P])
        r_gather = sb("r_gather", [P, 1], I32)
        r_scatter = sb("r_scatter", [P, 1], I32)
        r_gather_f = sb("r_gather_f", [P, 1])
        r_mask = sb("r_mask", [P, 1])
        r_count = sb("r_count", [P, 1])
        r_count_new = sb("r_count_new", [P, 1])
        r_inv = sb("r_inv", [P, 1])
        r_row = sb("r_row", [P, D])
        r_row_new = sb("r_row_new", [P, D])

        trans_ps = [pb(f"trans_ps{h}", [P, 2, 2, P]) for h in range(2)]
        z_ps = pb("z_ps", [P, 2, 512])
        sum_ps = pb("sum_ps", [P, TB, D + 1])
        cols_ps = pb("cols_ps", [P, 2, P])
        r_ps = pb("r_ps", [P, 2 * P])
        z_v = [z_ps[:, b, 0:2 * 2 * D].rearrange("p (j c) -> p j c", j=2) for b in range(2)]
        z_all = z_ps[:, :, 0:4 * D].rearrange("p b (j c) -> p b j c", j=2)

        def z4(a, b):
            return z_all[:, :, :, a:b]

        def as4(ap):
            return ap.rearrange("p (b j) c -> p b j c", b=2)

        s_const = sem("s_const")
        s_load = sem("s_load")
        s_pad = sem("s_pad")
        s_prep = sem("s_prep")
        s_cols = sem("s_cols")
        s_cols_out = sem("s_cols_out")
        s_viol = sem("s_viol")
        s_viol_ps = sem("s_viol_ps")
        s_flag = sem("s_flag")
        s_ones = sem("s_ones")
        node_loaded = sems("node_loaded")
        edge_loaded = sems("edge_loaded")
        across_loaded = sems("across_loaded")
        gathered = sems("gathered")
        node_stored = sems("node_stored")
        scattered = sems("scattered")
        gather_idx_ready = sem("gather_idx_ready")
        stats_done = sem("stats_done")
        parts_done = sem("parts_done")
        diff_sq_done = sem("diff_sq_done")
        var_done = sem("var_done")
        log_var_done = sem("log_var_done")
        rough_done = sem("rough_done")
        newton1_done = sem("newton1_done")
        newton2_done = sem("newton2_done")
        rstd_done = sem("rstd_done")
        shift_done = sem("shift_done")
        edge_norm_done = sem("edge_norm_done")
        node_norm_done = sem("node_norm_done")
        base_done = sem("base_done")
        node_sum_done = sem("node_sum_done")
        trans_done = [sem(f"trans_done{h}") for h in range(2)]
        trans_out = [sem(f"trans_out{h}") for h in range(2)]
        z_done = sem("z_done")
        relu_done = sem("relu_done")
        abs_done = sem("abs_done")
        exp_done = sem("exp_done")
        log_done = sem("log_done")
        softplus_done = sem("softplus_done")
        gate_den_done = sem("gate_den_done")
        gate_done = sem("gate_done")
        message_done = sem("message_done")
        same_done = sem("same_done")
        sum_done = sem("sum_done")
        count_done = sem("count_done")
        inv_done = sem("inv_done")
        final_done = sem("final_done")
        pool_go = sem("pool_go")
        r_zeroed = sem("r_zeroed")
        r_written = sem("r_written")
        r_diag_done = sem("r_diag_done")
        r_across_done = sem("r_across_done")
        r_same_done = sem("r_same_done")
        r_later_done = sem("r_later_done")
        r_sum_done = sem("r_sum_done")
        r_mask_done = sem("r_mask_done")
        r_idx_done = sem("r_idx_done")
        r_gathered = sem("r_gathered")
        r_clamped = sem("r_clamped")
        r_inv_done = sem("r_inv_done")
        r_new_done = sem("r_new_done")

        block = ctx.enter_context(nc.Block())

        def steps(eng, step, tail, peeled=1):
            for i in range(NS * peeled):
                step(i, i // NS, i % NS)
            with eng.Fori(peeled, OUTER) as o:
                for u in range(NS):
                    step(o * NS + u, o, u)
            for i in range(STEPS - 1, STEPS + tail):
                step(i, i // NS, i % NS)

        def back(i, o, u, n):
            return i - n, o - (1 if n % NS > u else 0) - n // NS, (u - n) % NS

        def runs_step(i):
            return not isinstance(i, int) or 0 <= i < STEPS

        def wait(eng, semaphore, value):
            if not isinstance(value, int) or value > 0:
                eng.wait_ge(semaphore, value)

        def chunk_of(t, i):
            if isinstance(i, int):
                first = min(i * CHUNK, NODES - CHUNK)
                return t[first:first + CHUNK, :].rearrange("(p r) d -> p r d", p=P)
            v = t[0:(STEPS - 1) * CHUNK, :].rearrange("(c p r) d -> c p r d", p=P, r=R)
            return v[bass.ds(i, 1), :, :, :].rearrange("a p r d -> (a p) r d")

        WHOLE = (STEPS - 1) * TB * P

        @block.sync
        def _(sp):
            sp.wait_ge(s_pad, 1)
            half = P * P
            full = (TILES - 1) * P
            for n, (t, shift_by) in enumerate(((dst, 0), (dst, 1), (src, 0))):
                sp.dma_start(index_rows[:, n, 0, :], t[shift_by:shift_by + half].rearrange("(t e) -> t e", e=P)).then_inc(s_load, 16)
                sp.dma_start(index_rows[0:TILES - 1 - P, n, 1, :],
                             t[half + shift_by:full + shift_by].rearrange("(t e) -> t e", e=P)).then_inc(s_load, 16)
                k = LAST_EDGES - shift_by
                sp.dma_start(index_rows[TILES - 1 - P:TILES - P, n, 1, 0:k],
                             t[full + shift_by:EDGES].rearrange("(a e) -> a e", a=1)).then_inc(s_load, 16)

            def step(i, o, u):
                j, oj, uj = back(i, o, u, NS)
                if runs_step(j):
                    wait(sp, node_sum_done, j + 1)
                    if isinstance(j, int) and j == STEPS - 1:
                        sp.wait_ge(node_stored[(j - 1) % NS], 16 * ((j - 1) // NS + 1))
                    sp.dma_start(chunk_of(out, j), node_out[uj][:, :, :]).then_inc(node_stored[uj], 16)
                if runs_step(i):
                    sp.dma_start(node_x[u][:, :, :], chunk_of(x, i)).then_inc(node_loaded[u], 16)
                    wait(sp, trans_done[1], i - NS + 1)
                    wait(sp, same_done, i - NS + 1)
                    if isinstance(i, int) and i == STEPS - 1:
                        t0, m = WHOLE, (TB - 1) * P
                        sp.dma_start(concat[u][:, 0:TB - 1, 2 * D:IN],
                                     edge_attr[t0:t0 + m, :].rearrange("(t p) f -> p t f", p=P)).then_inc(edge_loaded[u], 16)
                        sp.dma_start(concat[u][0:LAST_EDGES, TB - 1, 2 * D:IN],
                                     edge_attr[t0 + m:EDGES, :]).then_inc(edge_loaded[u], 16)
                        a = dst_across[u][:, :, :].rearrange("p t e -> p (t e)")
                        sp.dma_start(a[:, 0:EDGES - t0], dst[t0:EDGES].partition_broadcast(P)).then_inc(across_loaded[u], 16)
                    else:
                        ev = edge_attr[0:WHOLE, :].rearrange("(b t p) f -> b p t f", t=TB, p=P)
                        dv = dst[0:WHOLE].rearrange("(b e) -> b e", e=TB * P)
                        if isinstance(i, int):
                            e_src, d_src = ev[i, :, :, :], dv[i, :]
                        else:
                            e_src = ev[bass.ds(i, 1), :, :, :].rearrange("a p t f -> (a p) t f")
                            d_src = dv[bass.ds(i, 1), :].rearrange("a e -> (a e)")
                        sp.dma_start(concat[u][:, :, 2 * D:IN], e_src).then_inc(edge_loaded[u], 16)
                        sp.dma_start(dst_across[u][:, :, :].rearrange("p t e -> p (t e)"),
                                     d_src.partition_broadcast(P)).then_inc(across_loaded[u], 16)

            steps(sp, step, NS)
            for u in range(NS):
                sp.wait_ge(node_stored[u], 16 * ((STEPS - 1 - u) // NS + 1))

        @block.gpsimd
        def _(pool):
            nc.gpsimd.memset(ident[:, :], 0.0).then_inc(s_const, 1)
            nc.gpsimd.memset(ones[:, :], 1.0).then_inc(s_const, 1)
            for b in range(2):
                nc.gpsimd.iota(limit_i[:, b:b + 1], pattern=[[0, 1]], base=(CHUNK // TB) * P * b + SLACK,
                               channel_multiplier=CHUNK // TB).then_inc(s_const, 1)
            pool.wait_ge(s_const, 4)
            nc.gpsimd.affine_select(out=ident[:, :], in_=ident[:, :], compare_op=ALU.not_equal, fill=1.0, base=0,
                                    pattern=[[-1, P]], channel_multiplier=1).then_inc(s_const, 1)
            nc.gpsimd.affine_select(out=later[:, :], in_=ones[:, :], compare_op=ALU.is_gt, fill=0.0, base=0,
                                    pattern=[[-1, P]], channel_multiplier=1).then_inc(s_const, 1)

            def step(i, o, u):
                if runs_step(i):
                    wait(pool, gather_idx_ready, i + 1)
                    wait(pool, base_done, i - NS + 1)
                    pool.sem_inc(pool_go, 1)
                    for t in range(TB):
                        for side in range(2):
                            nc.gpsimd.indirect_dma_start(
                                out=edge_x[u][:, t, side, :], out_offset=None, in_=x,
                                in_offset=bass.IndirectOffsetOnAxis(ap=gather_idx[u][:, t, side:side + 1], axis=0),
                            ).then_inc(gathered[u], 16)
                lag = NS + AHEAD
                j, oj, uj = back(i, o, u, lag)
                if runs_step(j):
                    wait(pool, final_done, j + 1)
                    for n in range(NS):
                        c, oc, uc = back(i, o, u, lag - AHEAD + n)
                        if runs_step(c):
                            pool.wait_ge(node_stored[uc], oc * 16 + 16)
                    pool.sem_inc(pool_go, 1)
                    for t in range(TB):
                        nc.gpsimd.indirect_dma_start(
                            out=out, in_=final[uj][:, t, :], in_offset=None,
                            out_offset=bass.IndirectOffsetOnAxis(ap=scatter_idx[uj][:, t:t + 1], axis=0),
                            bounds_check=NODES - 1, oob_is_err=False).then_inc(scattered[uj], 16)

            steps(pool, step, NS + AHEAD, peeled=2)
            for u in range(NS):
                pool.wait_ge(scattered[u], 16 * TB * ((STEPS - 1 - u) // NS + 1))

            pool.wait_ge(s_flag, 1)
            bad = pool.value_load(flag[0:1, 0:1], min_val=0, max_val=1)
            with pool.If(bad != 0):
                pool.wait_ge(r_zeroed, 1)
                pool.dma_start(count_table.rearrange("(p n) a -> p (n a)", p=80), zeros[:, :]).then_inc(r_written, 16)
                with pool.Fori(0, TILES) as t:
                    pool.wait_ge(r_idx_done, t + 1)
                    pool.sem_inc(pool_go, 1)
                    nc.gpsimd.indirect_dma_start(out=r_count[:, :], out_offset=None, in_=count_table,
                                                 in_offset=bass.IndirectOffsetOnAxis(ap=r_gather[:, :], axis=0)
                                                 ).then_inc(r_gathered, 16)
                    pool.wait_ge(r_new_done, t + 1)
                    pool.sem_inc(pool_go, 1)
                    nc.gpsimd.indirect_dma_start(out=count_table, in_=r_count_new[:, :], in_offset=None,
                                                 out_offset=bass.IndirectOffsetOnAxis(ap=r_scatter[:, :], axis=0),
                                                 bounds_check=NODES - 1, oob_is_err=False).then_inc(r_written, 16)
                    pool.wait_ge(r_written, t * 16 + 32)
                with pool.Fori(0, TILES) as t:
                    pool.wait_ge(r_idx_done, t + TILES + 1)
                    pool.sem_inc(pool_go, 1)
                    nc.gpsimd.indirect_dma_start(out=r_count[:, :], out_offset=None, in_=count_table,
                                                 in_offset=bass.IndirectOffsetOnAxis(ap=r_gather[:, :], axis=0)
                                                 ).then_inc(r_gathered, 16)
                    nc.gpsimd.indirect_dma_start(out=r_row[:, :], out_offset=None, in_=out,
                                                 in_offset=bass.IndirectOffsetOnAxis(ap=r_gather[:, :], axis=0)
                                                 ).then_inc(r_gathered, 16)
                    pool.wait_ge(r_new_done, t + TILES + 1)
                    pool.sem_inc(pool_go, 1)
                    nc.gpsimd.indirect_dma_start(out=out, in_=r_row_new[:, :], in_offset=None,
                                                 out_offset=bass.IndirectOffsetOnAxis(ap=r_scatter[:, :], axis=0),
                                                 bounds_check=NODES - 1, oob_is_err=False).then_inc(r_written, 16)
                    pool.wait_ge(r_written, t * 16 + 16 * TILES + 32)

        @block.scalar
        def _(act):
            for n, w in enumerate((w_e, w_n)):
                act.dma_start(weights[:, :, n * D:(n + 1) * D], w.rearrange("(b p) d -> p b d", p=P)).then_inc(s_load, 16)
            for n, b in enumerate((b_e, b_n)):
                act.dma_start(bias[:, n * D:(n + 1) * D], b.rearrange("(a d) -> a d", a=1)).then_inc(s_load, 16)

            def norm_nodes(i, o, u, lo, hi):
                last = None
                for r in range(lo, hi):
                    c = 2 * TB + r
                    last = nc.scalar.activation(node_out[u][:, r, :], node_x[u][:, r, :], ACT.Relu,
                                                bias=shift[u][:, c:c + 1], scale=rstd[u][:, c:c + 1])
                return last

            def step(i, o, u):
                if runs_step(i):
                    wait(act, var_done, i + 1)
                    nc.scalar.activation(log_var[:, :], var96[:, :], ACT.Ln, scale=1.0 / D).then_inc(log_var_done, 1)
                    wait(act, log_var_done, i + 1)
                    nc.scalar.activation(rough[:, :], log_var[:, :], ACT.Exp, scale=-0.5).then_inc(rough_done, 1)
                j, oj, uj = back(i, o, u, 1)
                if runs_step(j):
                    wait(act, z_done, j + 1)
                    wait(act, softplus_done, j)
                    nc.scalar.activation(as4(relu_n[:, :, :]), z4(D, 2 * D), ACT.Relu).then_inc(relu_done, 1)
                    nc.scalar.activation(z4(D, 2 * D), z4(D, 2 * D), ACT.Abs).then_inc(abs_done, 1)
                    wait(act, abs_done, j + 1)
                    wait(act, gate_den_done, j)
                    nc.scalar.activation(as4(exp_both[:, :, :]), z4(0, 2 * D), ACT.Exp, scale=-1.0).then_inc(exp_done, 1)
                    wait(act, exp_done, j + 1)
                    nc.scalar.activation(log_n[:, :, :], exp_both[:, :, D:2 * D], ACT.Ln, bias=1.0).then_inc(log_done, 1)
                if runs_step(i):
                    wait(act, shift_done, i + 1)
                    wait(act, trans_done[1], i - NS + 1)
                    for t in range(TB):
                        for side in range(2):
                            c = 2 * t + side
                            last = nc.scalar.activation(concat[u][:, t, side * D:(side + 1) * D], edge_x[u][:, t, side, :],
                                                        ACT.Relu, bias=shift[u][:, c:c + 1], scale=rstd[u][:, c:c + 1])
                    last.then_inc(edge_norm_done, 1)
                    wait(act, node_stored[u], o * 16)
                    norm_nodes(i, o, u, 0, R // 2)
                    for h in range(2):
                        wait(act, trans_done[h], i + 1)
                        nc.scalar.activation(concat_t[:, h, :, :, :], trans_ps[h][:, :, :, :], ACT.Copy).then_inc(trans_out[h], 1)
                    norm_nodes(i, o, u, R // 2, R).then_inc(node_norm_done, 1)

            steps(act, step, 1)

        @block.vector
        def _(dve):
            nc.vector.memset(index_rows[:, 0:2, :, :], int(PAD))
            nc.vector.memset(index_rows[:, 2, :, :], 0).then_inc(s_pad, 1)
            nc.vector.memset(dst_col[:, 0:1], -1.0).then_inc(s_pad, 1)
            nc.vector.memset(gather_f[:, TILES:, :], 0.0)
            nc.vector.memset(messages[:, :, D:D + 1], 1.0).then_inc(s_ones, 1)
            dve.wait_ge(s_load, 16 * 13)
            dve.wait_ge(s_const, 6)
            chain = [0]

            def link(ins):
                chain[0] += 1
                ins.then_inc(s_prep, 1)
                dve.wait_ge(s_prep, chain[0])

            nc.vector.tensor_copy(limit[:, :], limit_i[:, :])
            link(nc.vector.tensor_copy(index_rows_f[:, :, :, :], index_rows[:, :, :, :]))
            dst_r, next_r = index_rows_f[:, 0, :, :], index_rows_f[:, 1, :, :]
            nc.vector.tensor_tensor(broken[:, :, :], dst_r, next_r, ALU.is_gt)
            link(nc.vector.tensor_scalar(real[:, :, :], dst_r, PAD, None, ALU.is_lt))
            for b in range(2):
                last = nc.vector.scalar_tensor_tensor(out=ahead[:, b, :], in0=dst_r[:, b, :], scalar=limit[:, b:b + 1],
                                                      in1=real[:, b, :], op0=ALU.is_ge, op1=ALU.mult)
            link(nc.vector.tensor_tensor(runs[:, :], dst_r[:, :, 0], dst_r[:, :, P - 1], ALU.is_equal))
            link(nc.vector.tensor_tensor(broken[:, :, :], broken[:, :, :], ahead[:, :, :], ALU.add))
            link(nc.vector.tensor_tensor(runs[:, :], runs[:, :], real[:, :, 0], ALU.mult))
            nc.vector.tensor_reduce(broken_sum[:, :], broken[:, :, :], AX.XY, ALU.add)
            link(nc.vector.tensor_reduce(runs_sum[:, :], runs[:, :], AX.X, ALU.add))
            nc.vector.tensor_tensor(violations[:, :], broken_sum[:, :], runs_sum[:, :], ALU.add).then_inc(s_viol, 1)
            cols = cols_ps[:, :, :].rearrange("p b e -> p (b e)")
            dve.wait_ge(s_cols, 1)
            nc.vector.tensor_copy(dst_col[:, 1:1 + TILES], cols[:, 0:TILES]).then_inc(s_cols_out, 1)
            dve.wait_ge(s_cols_out, 1)
            nc.vector.tensor_scalar(gather_f[:, 0:TILES, 1], dst_col[:, 1:1 + TILES], float(NODES - 1), None, ALU.min)
            dve.wait_ge(s_cols, 2)
            nc.vector.tensor_tensor(next_col[:, :], dst_col[:, 1:1 + TILES], cols[:, 0:TILES], ALU.is_equal).then_inc(s_cols_out, 1)
            dve.wait_ge(s_cols, 3)
            link(nc.vector.tensor_copy(gather_f[:, 0:TILES, 0], cols[:, 0:TILES]))
            dve.wait_ge(s_viol_ps, 1)
            link(nc.vector.tensor_scalar(skip[:, :], r_ps[:, 0:1], 0.5, None, ALU.is_gt))
            nc.vector.tensor_copy(flag[:, :], skip[:, :]).then_inc(s_flag, 1)
            link(nc.vector.tensor_scalar(next_col[:, :], next_col[:, :], skip[:, 0:1], PAD, ALU.max, ALU.mult))
            link(nc.vector.tensor_tensor(scatter_f[:, :], next_col[:, :], dst_col[:, 1:1 + TILES], ALU.add))

            def gather_columns(i, u):
                cols4 = bass.ds(i * TB, TB) if not isinstance(i, int) else slice(i * TB, (i + 1) * TB)
                nc.vector.tensor_copy(gather_idx[u][:, :, :], gather_f[:, cols4, :]).then_inc(gather_idx_ready, 1)

            for u in range(NS):
                gather_columns(u, u)

            def tiles_of(i, first=0):
                if isinstance(i, int):
                    return slice(i * TB + first, i * TB + first + TB)
                return bass.ds(i * TB + first, TB)

            def step(i, o, u):
                if runs_step(i):
                    dve.wait_ge(gathered[u], o * (16 * 2 * TB) + 16 * 2 * TB)
                    n = i + NS
                    if not isinstance(n, int) or n < STEPS:
                        gather_columns(n, u)
                    for r in range(2 * TB):
                        nc.vector.bn_stats(stats[:, r, :], edge_x[u][:, r // 2, r % 2, :])
                    dve.wait_ge(node_loaded[u], o * 16 + 16)
                    for r in range(R):
                        last = nc.vector.bn_stats(stats[:, 2 * TB + r, :], node_x[u][:, r, :])
                    last.then_inc(stats_done, 1)
                    wait(dve, stats_done, i + 1)
                    nc.vector.tensor_tensor(half_diff[:, :], stats[:, :, 1], stats[:, :, 4], ALU.subtract).then_inc(parts_done, 1)
                    nc.vector.scalar_tensor_tensor(out=sq_sum[:, :], in0=stats[:, :, 2], scalar=D * EPS, in1=stats[:, :, 5],
                                                   op0=ALU.add, op1=ALU.add).then_inc(parts_done, 1)
                    nc.vector.tensor_tensor(mean2[u][:, :], stats[:, :, 1], stats[:, :, 4], ALU.add).then_inc(parts_done, 1)
                    wait(dve, parts_done, i * 3 + 3)
                    nc.vector.tensor_tensor(diff_sq[:, :], half_diff[:, :], half_diff[:, :], ALU.mult).then_inc(diff_sq_done, 1)
                    wait(dve, diff_sq_done, i + 1)
                    nc.vector.scalar_tensor_tensor(out=var96[:, :], in0=diff_sq[:, :], scalar=D / 4.0, in1=sq_sum[:, :],
                                                   op0=ALU.mult, op1=ALU.add).then_inc(var_done, 1)
                j, oj, uj = back(i, o, u, 2)
                if runs_step(j):
                    wait(dve, sum_done, j + 1)
                    nc.vector.tensor_scalar(count[:, :], sum_ps[:, :, D], 1.0, None, ALU.max).then_inc(count_done, 1)
                    wait(dve, count_done, j + 1)
                    nc.vector.reciprocal(inv_count[:, :], count[:, :]).then_inc(inv_done, 1)
                    wait(dve, scattered[uj], oj * (16 * TB))
                    nc.vector.tensor_copy(scatter_idx[uj][:, :], scatter_f[:, tiles_of(j)])
                    wait(dve, inv_done, j + 1)
                    for t in range(TB):
                        last = nc.vector.scalar_tensor_tensor(out=final[uj][:, t, :], in0=sum_ps[:, t, 0:D],
                                                              scalar=inv_count[:, t:t + 1], in1=base[uj][:, t, :],
                                                              op0=ALU.mult, op1=ALU.add)
                    last.then_inc(final_done, 1)
                j, oj, uj = back(i, o, u, 1)
                if runs_step(j):
                    rounds = oj + 1
                    wait(dve, across_loaded[uj], rounds * 16)
                    for prev in range(2):
                        k = dst_col[:, tiles_of(j, 1 - prev)].unsqueeze(2).to_broadcast([P, TB, P])
                        last = nc.vector.tensor_tensor(same[:, prev, :, :], dst_across[uj][:, :, :], k, ALU.is_equal)
                    last.then_inc(same_done, 1)
                if runs_step(i):
                    wait(dve, rough_done, i + 1)
                    nc.vector.tensor_tensor(rough_sq[:, :], rough[:, :], rough[:, :], ALU.mult).then_inc(newton1_done, 1)
                    wait(dve, newton1_done, i + 1)
                    nc.vector.scalar_tensor_tensor(out=correction[:, :], in0=rough_sq[:, :], scalar=-0.5 / D, in1=var96[:, :],
                                                   op0=ALU.mult, op1=ALU.mult).then_inc(newton2_done, 1)
                    wait(dve, newton2_done, i + 1)
                    nc.vector.scalar_tensor_tensor(out=rstd[u][:, :], in0=correction[:, :], scalar=1.5, in1=rough[:, :],
                                                   op0=ALU.add, op1=ALU.mult).then_inc(rstd_done, 1)
                    wait(dve, rstd_done, i + 1)
                    nc.vector.scalar_tensor_tensor(out=shift[u][:, :], in0=mean2[u][:, :], scalar=-0.5, in1=rstd[u][:, :],
                                                   op0=ALU.mult, op1=ALU.mult).then_inc(shift_done, 1)
                if runs_step(j):
                    wait(dve, edge_norm_done, j + 1)
                    nc.vector.tensor_tensor(base[uj][:, :, :], edge_x[uj][:, :, 1, :], concat[uj][:, :, D:2 * D],
                                            ALU.add).then_inc(base_done, 1)
                    wait(dve, node_norm_done, j + 1)
                    nc.vector.tensor_tensor(node_out[uj][:, :, :], node_out[uj][:, :, :], node_x[uj][:, :, :],
                                            ALU.add).then_inc(node_sum_done, 1)
                    wait(dve, exp_done, j + 1)
                    nc.vector.tensor_scalar(gate_den[:, :, :], exp_both[:, :, 0:D], 1.0, None, ALU.add).then_inc(gate_den_done, 1)
                    wait(dve, gate_den_done, j + 1)
                    nc.vector.reciprocal(gate[:, :, :], gate_den[:, :, :]).then_inc(gate_done, 1)
                    wait(dve, log_done, j + 1)
                    nc.vector.tensor_tensor(softplus[:, :, :], relu_n[:, :, :], log_n[:, :, :], ALU.add).then_inc(softplus_done, 1)
                    wait(dve, softplus_done, j + 1)
                    nc.vector.tensor_tensor(messages[:, tiles_of(j), 0:D], gate[:, :, :], softplus[:, :, :],
                                            ALU.mult).then_inc(message_done, 1)

            steps(dve, step, 2, peeled=2)

            bad = dve.value_load(flag[0:1, 0:1], min_val=0, max_val=1)

            def tile_indices(t, n):
                dst_t = dst_col[:, bass.ds(t + 1, 1)]
                dve.wait_ge(r_written, n * 16 + 16)
                nc.vector.tensor_scalar(diag[:, :], ident[:, :], dst_t, None, ALU.mult).then_inc(r_diag_done, 1)
                dve.wait_ge(r_across_done, n + 1)
                nc.vector.tensor_scalar(r_same[:, :], r_ps[:, P:2 * P], dst_t, None, ALU.is_equal).then_inc(r_same_done, 1)
                dve.wait_ge(r_same_done, n + 1)
                nc.vector.tensor_tensor(r_later[:, :], r_same[:, :], later[:, :], ALU.mult).then_inc(r_later_done, 1)
                dve.wait_ge(r_sum_done, n + 1)
                nc.vector.tensor_scalar(r_mask[:, :], r_ps[:, D + 1:D + 2], 0.5, PAD, ALU.is_gt, ALU.mult).then_inc(r_mask_done, 1)
                nc.vector.tensor_scalar(r_gather_f[:, :], dst_t, float(NODES - 1), None, ALU.min).then_inc(r_mask_done, 1)
                dve.wait_ge(r_mask_done, n * 2 + 2)
                nc.vector.tensor_copy(r_gather[:, :], r_gather_f[:, :])
                nc.vector.tensor_tensor(r_scatter[:, :], r_mask[:, :], dst_t, ALU.add).then_inc(r_idx_done, 1)

            with dve.If(bad != 0):
                nc.vector.memset(zeros[:, :], 0.0).then_inc(r_zeroed, 1)
                with dve.Fori(0, TILES) as t:
                    tile_indices(t, t)
                    dve.wait_ge(r_gathered, t * 16 + 16)
                    nc.vector.tensor_tensor(r_count_new[:, :], r_count[:, :], r_ps[:, D:D + 1], ALU.add).then_inc(r_new_done, 1)
                with dve.Fori(0, TILES) as t:
                    tile_indices(t, t + TILES)
                    dve.wait_ge(r_gathered, t * 32 + 16 * TILES + 32)
                    nc.vector.tensor_scalar(r_count_new[:, :], r_count[:, :], 1.0, None, ALU.max).then_inc(r_clamped, 1)
                    dve.wait_ge(r_clamped, t + 1)
                    nc.vector.reciprocal(r_inv[:, :], r_count_new[:, :]).then_inc(r_inv_done, 1)
                    dve.wait_ge(r_inv_done, t + 1)
                    nc.vector.scalar_tensor_tensor(out=r_row_new[:, :], in0=r_ps[:, 0:D], scalar=r_inv[:, 0:1], in1=r_row[:, :],
                                                   op0=ALU.mult, op1=ALU.add).then_inc(r_new_done, 1)

        @block.tensor
        def _(pe):
            pe.wait_ge(s_const, 6)
            pe.wait_ge(s_prep, 1)
            for n, row in enumerate((0, 1, 2)):
                if n:
                    pe.wait_ge(s_cols_out, n)
                nc.tensor.transpose(cols_ps[:, 0, :], index_rows_f[:, row, 0, :], ident[:, :])
                k = TILES - P
                nc.tensor.transpose(cols_ps[:, 1, 0:k], index_rows_f[0:k, row, 1, :], ident[0:k, 0:k]).then_inc(s_cols, 1)
            pe.wait_ge(s_viol, 1)
            nc.tensor.matmul(r_ps[:, 0:1], ones[:, :], violations[:, :], start=True, stop=True).then_inc(s_viol_ps, 1)
            pe.wait_ge(s_ones, 1)
            pe.wait_ge(s_load, 16 * 13)

            def step(i, o, u):
                if runs_step(i):
                    wait(pe, edge_norm_done, i + 1)
                    if isinstance(i, int) and i == STEPS - 1:
                        pe.wait_ge(edge_loaded[u], o * 16 + 32)
                    else:
                        pe.wait_ge(edge_loaded[u], o * 16 + 16)
                    for h in range(2):
                        wait(pe, trans_out[h], i)
                        for t in range(2):
                            for b in range(2):
                                last = nc.tensor.transpose(trans_ps[h][:, t, b, :], concat[u][:, 2 * h + t, b * P:(b + 1) * P],
                                                           ident[:, :])
                        last.then_inc(trans_done[h], 1)
                    wait(pe, exp_done, i)
                    for h in range(2):
                        wait(pe, trans_out[h], i + 1)
                        for t in range(2):
                            z = z_v[h][:, t, :]
                            nc.tensor.matmul(z, ones[0:1, :], bias[0:1, :], start=True, stop=False)
                            for b in range(2):
                                last = nc.tensor.matmul(z, concat_t[:, h, t, b, :], weights[:, b, :], start=False, stop=(b == 1))
                    last.then_inc(z_done, 1)
                j, oj, uj = back(i, o, u, 1)
                if runs_step(j):
                    wait(pe, message_done, j + 1)
                    wait(pe, same_done, j + 1)
                    wait(pe, final_done, j)
                    for t in range(TB):
                        if isinstance(j, int):
                            cur, prev = messages[:, j * TB + t, :], messages[:, max(j * TB + t - 1, 0), :]
                        else:
                            cur = messages[:, bass.ds(j * TB + t, 1), :].rearrange("p a c -> p (a c)")
                            prev = messages[:, bass.ds(j * TB + (t - 1), 1), :].rearrange("p a c -> p (a c)")
                        nc.tensor.matmul(sum_ps[:, t, :], same[:, 0, t, :], cur, start=True, stop=False)
                        last = nc.tensor.matmul(sum_ps[:, t, :], same[:, 1, t, :], prev, start=False, stop=True)
                    last.then_inc(sum_done, 1)

            steps(pe, step, 1)

            pe.wait_ge(s_flag, 1)
            bad = pe.value_load(flag[0:1, 0:1], min_val=0, max_val=1)

            def tile_sums(t, n):
                pe.wait_ge(r_diag_done, n + 1)
                nc.tensor.matmul(r_ps[:, P:2 * P], ones[:, :], diag[:, :], start=True, stop=True).then_inc(r_across_done, 1)
                pe.wait_ge(r_later_done, n + 1)
                m = messages[:, bass.ds(t, 1), :].rearrange("p a c -> p (a c)")
                nc.tensor.matmul(r_ps[:, 0:D + 1], r_same[:, :], m, start=True, stop=True)
                nc.tensor.matmul(r_ps[:, D + 1:D + 2], r_later[:, :], ones[:, 0:1], start=True, stop=True).then_inc(r_sum_done, 1)

            with pe.If(bad != 0):
                with pe.Fori(0, TILES) as t:
                    tile_sums(t, t)
                with pe.Fori(0, TILES) as t:
                    tile_sums(t, t + TILES)


_INS = ["x", "src", "dst", "edge_attr_64", "L0_gnn_W_e", "L0_gnn_b_e", "L0_gnn_W_n", "L0_gnn_b_n"]


def kernel(**inputs):
    import numpy as _np
    import concourse.bacc as _bacc
    from concourse import mybir as _mybir
    from concourse.bass_utils import run_bass_kernel_spmd as _run

    nc = _bacc.Bacc("TRN2", target_bir_lowering=False, num_devices=1)
    arrays, args = {}, []
    for name in _INS:
        a = _np.ascontiguousarray(inputs[name])
        arrays[f"in_{name}"] = a
        args.append(nc.dram_tensor(f"in_{name}", a.shape, _mybir.dt.from_np(a.dtype), kind="ExternalInput").ap())
    out = nc.dram_tensor("out", (NODES, D), FP32, kind="ExternalOutput").ap()
    count_table = nc.dram_tensor("count_table", (NODES, 1), FP32, kind="Internal").ap()
    build(nc, *args, out, count_table)
    return _run(nc, [arrays], core_ids=[0]).results[0]["out"]
```

```python
import concourse.bass as bass
from concourse import mybir
from contextlib import ExitStack

FP32 = mybir.dt.float32
I32 = mybir.dt.int32
ALU = mybir.AluOpType
ACT = mybir.ActivationFunctionType
AX = mybir.AxisListType

P = 128
NODES, D = 100000, 96
EDGES, DE = 25000, 64
IN = 2 * D + DE
TILES = -(-EDGES // P)
TB = 4
STEPS = TILES // TB
LAST_EDGES = EDGES - (TILES - 1) * P
R = 16
CHUNK = P * R
ROWS = 2 * TB + R
NS = 4
OUTER = (STEPS - 1) // NS
BY_DVE = 2
PAD = float(1 << 20)
AHEAD = 2
EPS = 1e-5
SLACK = AHEAD * CHUNK - (TB - 1) * (CHUNK // TB)
assert STEPS * TB == TILES and OUTER * NS + 1 == STEPS and STEPS * CHUNK >= NODES > (STEPS - 1) * CHUNK


def build(nc, x, src, dst, edge_attr, w_e, b_e, w_n, b_n, out, count_table):
    ctx = ExitStack()
    with ctx:
        def sb(name, shape, dt=FP32):
            return ctx.enter_context(nc.sbuf_tensor(name, shape, dt))

        def pb(name, shape):
            return ctx.enter_context(nc.psum_tensor(name, shape, FP32))

        def sem(name):
            return ctx.enter_context(nc.semaphore(name))

        def sems(name):
            return [sem(f"{name}{u}") for u in range(NS)]

        ident = sb("ident", [P, P])
        ones = sb("ones", [P, P])
        later = sb("later", [P, P])
        weights = sb("weights", [P, 2, 2 * D])
        bias = sb("bias", [1, 2 * D])
        index_rows = sb("index_rows", [P, 3, 2, P], I32)
        index_rows_f = sb("index_rows_f", [P, 3, 2, P])
        limit_i = sb("limit_i", [P, 2], I32)
        limit = sb("limit", [P, 2])
        real = sb("real", [P, 2, P])
        broken = sb("broken", [P, 2, P])
        ahead = sb("ahead", [P, 2, P])
        runs = sb("runs", [P, 2])
        broken_sum = sb("broken_sum", [P, 1])
        runs_sum = sb("runs_sum", [P, 1])
        violations = sb("violations", [P, 1])
        skip = sb("skip", [P, 1])
        flag = sb("flag", [P, 1], I32)
        dst_col = sb("dst_col", [P, 1 + TILES])
        next_col = sb("next_col", [P, TILES])
        gather_f = sb("gather_f", [P, TILES + (NS - 1) * TB, 2])
        scatter_f = sb("scatter_f", [P, TILES])
        gather_idx = [sb(f"gather_idx{u}", [P, TB, 2], I32) for u in range(NS)]
        scatter_idx = [sb(f"scatter_idx{u}", [P, TB], I32) for u in range(NS)]
        node_x = [sb(f"node_x{u}", [P, R, D]) for u in range(NS)]
        node_out = [sb(f"node_out{u}", [P, R, D]) for u in range(NS)]
        edge_x = [sb(f"edge_x{u}", [P, TB, 2, D]) for u in range(NS)]
        concat = [sb(f"concat{u}", [P, TB, IN]) for u in range(NS)]
        dst_across = [sb(f"dst_across{u}", [P, TB, P], I32) for u in range(NS)]
        base = [sb(f"base{u}", [P, TB, D]) for u in range(2)]
        final = [sb(f"final{u}", [P, TB, D]) for u in range(NS)]
        rstd = [sb(f"rstd{u}", [P, ROWS]) for u in range(NS)]
        shift = [sb(f"shift{u}", [P, ROWS]) for u in range(NS)]
        stats = sb("stats", [P, ROWS, 6])
        half_diff = sb("half_diff", [P, ROWS])
        mean2 = [sb(f"mean2_{u}", [P, ROWS]) for u in range(NS)]
        sq_sum = sb("sq_sum", [P, ROWS])
        diff_sq = sb("diff_sq", [P, ROWS])
        var96 = sb("var96", [P, ROWS])
        log_var = sb("log_var", [P, ROWS])
        rough = sb("rough", [P, ROWS])
        rough_sq = sb("rough_sq", [P, ROWS])
        correction = sb("correction", [P, ROWS])
        concat_t = sb("concat_t", [P, 2, 2, 2, P])
        magnitude = sb("magnitude", [P, TB, 2 * D])
        log1p = sb("log1p", [P, TB, 2 * D])
        log_gate = sb("log_gate", [P, TB, D])
        gate = sb("gate", [P, TB, D])
        softplus = sb("softplus", [P, TB, D])
        same = sb("same", [P, 2, TB, P])
        count = sb("count", [P, TB])
        inv_count = sb("inv_count", [P, TB])
        messages = sb("messages", [P, TILES, D + 1])
        zeros = node_x[0][0:80, :, :].rearrange("p r d -> p (r d)")[:, 0:NODES // 80]
        diag = same[:, 0, 0, :]
        r_same = same[:, 0, 1, :]
        r_later = same[:, 0, 2, :]
        r_gather = sb("r_gather", [P, 1], I32)
        r_scatter = sb("r_scatter", [P, 1], I32)
        r_gather_f = sb("r_gather_f", [P, 1])
        r_mask = sb("r_mask", [P, 1])
        r_count = sb("r_count", [P, 1])
        r_count_new = sb("r_count_new", [P, 1])
        r_inv = sb("r_inv", [P, 1])
        r_row = sb("r_row", [P, D])
        r_row_new = sb("r_row_new", [P, D])

        trans_ps = [pb(f"trans_ps{h}", [P, 2, 2, P]) for h in range(2)]
        z_ps = [pb(f"z_ps{v}", [P, TB, 256]) for v in range(2)]
        sum_ps = pb("sum_ps", [P, TB, D + 1])
        side_ps = pb("side_ps", [P, 512])
        cols_ps = side_ps[:, 0:2 * P].rearrange("p (b e) -> p b e", b=2)
        r_ps = side_ps[:, 2 * P:4 * P]

        s_const = sem("s_const")
        s_load = sem("s_load")
        s_pad = sem("s_pad")
        s_prep = sem("s_prep")
        s_cols = sem("s_cols")
        s_cols_out = sem("s_cols_out")
        s_viol = sem("s_viol")
        s_viol_ps = sem("s_viol_ps")
        s_flag = sem("s_flag")
        s_ones = sem("s_ones")
        node_loaded = sems("node_loaded")
        edge_loaded = sems("edge_loaded")
        across_loaded = sems("across_loaded")
        gathered = sems("gathered")
        node_stored = sems("node_stored")
        scattered = sems("scattered")
        gather_idx_ready = sem("gather_idx_ready")
        stats_done = sem("stats_done")
        parts_done = sem("parts_done")
        diff_sq_done = sem("diff_sq_done")
        var_done = sem("var_done")
        log_var_done = sem("log_var_done")
        rough_done = sem("rough_done")
        newton1_done = sem("newton1_done")
        newton2_done = sem("newton2_done")
        rstd_done = sem("rstd_done")
        shift_done = sem("shift_done")
        edge_norm_done = sem("edge_norm_done")
        dve_norm_done = sem("dve_norm_done")
        node_norm_done = sem("node_norm_done")
        base_done = sem("base_done")
        node_sum_done = sem("node_sum_done")
        trans_done = [sem(f"trans_done{h}") for h in range(2)]
        trans_out = [sem(f"trans_out{h}") for h in range(2)]
        z_done = sem("z_done")
        magnitude_done = sem("magnitude_done")
        decay_done = sem("decay_done")
        log1p_done = sem("log1p_done")
        log_gate_done = sem("log_gate_done")
        softplus_done = sem("softplus_done")
        gate_done = sem("gate_done")
        message_done = sem("message_done")
        same_done = sem("same_done")
        sum_done = sem("sum_done")
        count_done = sem("count_done")
        inv_done = sem("inv_done")
        final_done = sem("final_done")
        pool_go = sem("pool_go")
        r_zeroed = sem("r_zeroed")
        r_written = sem("r_written")
        r_diag_done = sem("r_diag_done")
        r_across_done = sem("r_across_done")
        r_same_done = sem("r_same_done")
        r_later_done = sem("r_later_done")
        r_sum_done = sem("r_sum_done")
        r_mask_done = sem("r_mask_done")
        r_idx_done = sem("r_idx_done")
        r_gathered = sem("r_gathered")
        r_clamped = sem("r_clamped")
        r_inv_done = sem("r_inv_done")
        r_new_done = sem("r_new_done")

        block = ctx.enter_context(nc.Block())

        def steps(eng, step, tail, peeled=1):
            for i in range(NS * peeled):
                step(i, i // NS, i % NS)
            with eng.Fori(peeled, OUTER) as o:
                for u in range(NS):
                    step(o * NS + u, o, u)
            for i in range(STEPS - 1, STEPS + tail):
                step(i, i // NS, i % NS)

        def back(i, o, u, n):
            return i - n, o - (1 if n % NS > u else 0) - n // NS, (u - n) % NS

        def runs_step(i):
            return not isinstance(i, int) or 0 <= i < STEPS

        def ends(i, passed):
            return isinstance(i, int) and i >= STEPS + passed and i - 2 < STEPS

        def wait(eng, semaphore, value):
            if not isinstance(value, int) or value > 0:
                eng.wait_ge(semaphore, value)

        def chunk_of(t, i):
            if isinstance(i, int):
                first = min(i * CHUNK, NODES - CHUNK)
                return t[first:first + CHUNK, :].rearrange("(p r) d -> p r d", p=P)
            v = t[0:(STEPS - 1) * CHUNK, :].rearrange("(c p r) d -> c p r d", p=P, r=R)
            return v[bass.ds(i, 1), :, :, :].rearrange("a p r d -> (a p) r d")

        @block.sync
        def _(sp):
            sp.wait_ge(s_pad, 1)
            half = P * P
            full = (TILES - 1) * P
            for n, (t, shift_by) in enumerate(((dst, 0), (dst, 1), (src, 0))):
                sp.dma_start(index_rows[:, n, 0, :], t[shift_by:shift_by + half].rearrange("(t e) -> t e", e=P)).then_inc(s_load, 16)
                sp.dma_start(index_rows[0:TILES - 1 - P, n, 1, :],
                             t[half + shift_by:full + shift_by].rearrange("(t e) -> t e", e=P)).then_inc(s_load, 16)
                k = LAST_EDGES - shift_by
                sp.dma_start(index_rows[TILES - 1 - P:TILES - P, n, 1, 0:k],
                             t[full + shift_by:EDGES].rearrange("(a e) -> a e", a=1)).then_inc(s_load, 16)

            def step(i, o, u):
                j, oj, uj = back(i, o, u, NS)
                if runs_step(j):
                    wait(sp, node_sum_done, j + 1)
                    if isinstance(j, int) and j == STEPS - 1:
                        sp.wait_ge(node_stored[(j - 1) % NS], 16 * ((j - 1) // NS + 1))
                    sp.dma_start(chunk_of(out, j), node_out[uj][:, :, :]).then_inc(node_stored[uj], 16)
                tail = (STEPS - 1) * TB * P
                if runs_step(i):
                    sp.dma_start(node_x[u][:, :, :], chunk_of(x, i)).then_inc(node_loaded[u], 16)
                    wait(sp, trans_done[1], i - NS + 1)
                    if isinstance(i, int) and i == STEPS - 1:
                        m = (TB - 1) * P
                        sp.dma_start(concat[u][:, 0:TB - 1, 2 * D:IN],
                                     edge_attr[tail:tail + m, :].rearrange("(t p) f -> p t f", p=P)).then_inc(edge_loaded[u], 16)
                        sp.dma_start(concat[u][0:LAST_EDGES, TB - 1, 2 * D:IN],
                                     edge_attr[tail + m:EDGES, :]).then_inc(edge_loaded[u], 16)
                    else:
                        ev = edge_attr[0:tail, :].rearrange("(b t p) f -> b p t f", t=TB, p=P)
                        e_src = ev[i, :, :, :] if isinstance(i, int) else ev[bass.ds(i, 1), :, :, :].rearrange("a p t f -> (a p) t f")
                        sp.dma_start(concat[u][:, :, 2 * D:IN], e_src).then_inc(edge_loaded[u], 16)
                k, ok, uk = back(i, o, u, 1)
                if runs_step(k):
                    wait(sp, same_done, k - NS + 1)
                    across = dst_across[uk][:, :, :].rearrange("p t e -> p (t e)")
                    dv = dst[0:tail].rearrange("(b e) -> b e", e=TB * P)
                    if isinstance(k, int) and k == STEPS - 1:
                        d_src, across = dst[tail:EDGES], across[:, 0:EDGES - tail]
                    else:
                        d_src = dv[k, :] if isinstance(k, int) else dv[bass.ds(k, 1), :].rearrange("a e -> (a e)")
                    sp.dma_start(across, d_src.partition_broadcast(P)).then_inc(across_loaded[uk], 16)

            steps(sp, step, NS)
            for u in range(NS):
                sp.wait_ge(node_stored[u], 16 * ((STEPS - 1 - u) // NS + 1))

        @block.gpsimd
        def _(pool):
            nc.gpsimd.memset(ident[:, :], 0.0).then_inc(s_const, 1)
            nc.gpsimd.memset(ones[:, :], 1.0).then_inc(s_const, 1)
            for b in range(2):
                nc.gpsimd.iota(limit_i[:, b:b + 1], pattern=[[0, 1]], base=(CHUNK // TB) * P * b + SLACK,
                               channel_multiplier=CHUNK // TB).then_inc(s_const, 1)
            pool.wait_ge(s_const, 4)
            nc.gpsimd.affine_select(out=ident[:, :], in_=ident[:, :], compare_op=ALU.not_equal, fill=1.0, base=0,
                                    pattern=[[-1, P]], channel_multiplier=1).then_inc(s_const, 1)
            nc.gpsimd.affine_select(out=later[:, :], in_=ones[:, :], compare_op=ALU.is_gt, fill=0.0, base=0,
                                    pattern=[[-1, P]], channel_multiplier=1).then_inc(s_const, 1)

            def step(i, o, u):
                if runs_step(i):
                    wait(pool, gather_idx_ready, i + 1)
                    wait(pool, base_done, i - NS + 1)
                    pool.sem_inc(pool_go, 1)
                    for t in range(TB):
                        for side in range(2):
                            nc.gpsimd.indirect_dma_start(
                                out=edge_x[u][:, t, side, :], out_offset=None, in_=x,
                                in_offset=bass.IndirectOffsetOnAxis(ap=gather_idx[u][:, t, side:side + 1], axis=0),
                            ).then_inc(gathered[u], 16)
                lag = NS + 2
                j, oj, uj = back(i, o, u, lag)
                if runs_step(j):
                    wait(pool, final_done, j + 1)
                    for n in range(AHEAD + 1 if isinstance(j, int) and j == 0 else 1):
                        c, oc, uc = back(i, o, u, lag - AHEAD + n)
                        if runs_step(c):
                            pool.wait_ge(node_stored[uc], oc * 16 + 16)
                    pool.sem_inc(pool_go, 1)
                    for t in range(TB):
                        nc.gpsimd.indirect_dma_start(
                            out=out, in_=final[uj][:, t, :], in_offset=None,
                            out_offset=bass.IndirectOffsetOnAxis(ap=scatter_idx[uj][:, t:t + 1], axis=0),
                            bounds_check=NODES - 1, oob_is_err=False).then_inc(scattered[uj], 16)

            steps(pool, step, NS + 2, peeled=2)
            for u in range(NS):
                pool.wait_ge(scattered[u], 16 * TB * ((STEPS - 1 - u) // NS + 1))

            pool.wait_ge(s_flag, 1)
            bad = pool.value_load(flag[0:1, 0:1], min_val=0, max_val=1)
            with pool.If(bad != 0):
                pool.wait_ge(r_zeroed, 1)
                pool.dma_start(count_table.rearrange("(p n) a -> p (n a)", p=80), zeros).then_inc(r_written, 16)
                with pool.Fori(0, TILES) as t:
                    pool.wait_ge(r_idx_done, t + 1)
                    pool.sem_inc(pool_go, 1)
                    nc.gpsimd.indirect_dma_start(out=r_count[:, :], out_offset=None, in_=count_table,
                                                 in_offset=bass.IndirectOffsetOnAxis(ap=r_gather[:, :], axis=0)
                                                 ).then_inc(r_gathered, 16)
                    pool.wait_ge(r_new_done, t + 1)
                    pool.sem_inc(pool_go, 1)
                    nc.gpsimd.indirect_dma_start(out=count_table, in_=r_count_new[:, :], in_offset=None,
                                                 out_offset=bass.IndirectOffsetOnAxis(ap=r_scatter[:, :], axis=0),
                                                 bounds_check=NODES - 1, oob_is_err=False).then_inc(r_written, 16)
                    pool.wait_ge(r_written, t * 16 + 32)
                with pool.Fori(0, TILES) as t:
                    pool.wait_ge(r_idx_done, t + TILES + 1)
                    pool.sem_inc(pool_go, 1)
                    nc.gpsimd.indirect_dma_start(out=r_count[:, :], out_offset=None, in_=count_table,
                                                 in_offset=bass.IndirectOffsetOnAxis(ap=r_gather[:, :], axis=0)
                                                 ).then_inc(r_gathered, 16)
                    nc.gpsimd.indirect_dma_start(out=r_row[:, :], out_offset=None, in_=out,
                                                 in_offset=bass.IndirectOffsetOnAxis(ap=r_gather[:, :], axis=0)
                                                 ).then_inc(r_gathered, 16)
                    pool.wait_ge(r_new_done, t + TILES + 1)
                    pool.sem_inc(pool_go, 1)
                    nc.gpsimd.indirect_dma_start(out=out, in_=r_row_new[:, :], in_offset=None,
                                                 out_offset=bass.IndirectOffsetOnAxis(ap=r_scatter[:, :], axis=0),
                                                 bounds_check=NODES - 1, oob_is_err=False).then_inc(r_written, 16)
                    pool.wait_ge(r_written, t * 16 + 16 * TILES + 32)

        @block.scalar
        def _(act):
            for n, w in enumerate((w_e, w_n)):
                act.dma_start(weights[:, :, n * D:(n + 1) * D], w.rearrange("(b p) d -> p b d", p=P)).then_inc(s_load, 16)
            for n, b in enumerate((b_e, b_n)):
                act.dma_start(bias[:, n * D:(n + 1) * D], b.rearrange("(a d) -> a d", a=1)).then_inc(s_load, 16)

            nc.scalar.preload_act_table_set("natural_log_exp_and_others")

            def norm_nodes(u, lo, hi):
                for r in range(lo, hi):
                    c = 2 * TB + r
                    last = nc.scalar.activation(node_out[u][:, r, :], node_x[u][:, r, :], ACT.Relu,
                                                bias=shift[u][:, c:c + 1], scale=rstd[u][:, c:c + 1])
                return last

            def sigmoid(n):
                wait(act, log_gate_done, n + 1)
                wait(act, message_done, n)
                nc.scalar.activation(gate[:, :, :], log_gate[:, :, :], ACT.Exp).then_inc(gate_done, 1)

            def step(i, o, u):
                k, ok, uk = back(i, o, u, 1)
                j, oj, uj = back(i, o, u, 2)
                m, om, um = back(i, o, u, 3)
                if runs_step(m) and not ends(i, 1):
                    sigmoid(m)
                if runs_step(k):
                    wait(act, shift_done, k + 1)
                    wait(act, trans_done[1], k - NS + 1)
                    wait(act, base_done, k - NS + 1)
                    for t in range(TB):
                        for side in range(2):
                            c = 2 * t + side
                            last = nc.scalar.activation(concat[uk][:, t, side * D:(side + 1) * D], edge_x[uk][:, t, side, :],
                                                        ACT.Relu, bias=shift[uk][:, c:c + 1], scale=rstd[uk][:, c:c + 1])
                    last.then_inc(edge_norm_done, 1)
                    wait(act, node_stored[uk], ok * 16)
                    norm_nodes(uk, 0, 4)
                if runs_step(k):
                    for h in range(2):
                        wait(act, trans_done[h], k + 1)
                        wait(act, z_done, k)
                        nc.scalar.activation(concat_t[:, h, :, :, :], trans_ps[h][:, :, :, :], ACT.Copy).then_inc(trans_out[h], 1)
                if runs_step(j):
                    wait(act, z_done, j + 1)
                    wait(act, log1p_done, j)
                    nc.scalar.activation(magnitude[:, :, :], z_ps[uj % 2][:, :, 0:2 * D], ACT.Abs).then_inc(magnitude_done, 1)
                if runs_step(k):
                    norm_nodes(uk, 4, 5)
                if runs_step(j):
                    wait(act, magnitude_done, j + 1)
                    nc.scalar.activation(magnitude[:, :, :], magnitude[:, :, :], ACT.Exp, scale=-1.0).then_inc(decay_done, 1)
                if runs_step(k):
                    norm_nodes(uk, 5, 6)
                if runs_step(j):
                    wait(act, decay_done, j + 1)
                    wait(act, softplus_done, j)
                    nc.scalar.activation(log1p[:, :, :], magnitude[:, :, :], ACT.Ln, bias=1.0).then_inc(log1p_done, 1)
                if runs_step(k):
                    norm_nodes(uk, 6, R - BY_DVE - 3)
                if runs_step(i):
                    wait(act, var_done, i + 1)
                    nc.scalar.activation(log_var[:, :], var96[:, :], ACT.Ln, scale=1.0 / D).then_inc(log_var_done, 1)
                if runs_step(k):
                    norm_nodes(uk, R - BY_DVE - 3, R - BY_DVE - 2)
                if runs_step(i):
                    wait(act, log_var_done, i + 1)
                    nc.scalar.activation(rough[:, :], log_var[:, :], ACT.Exp, scale=-0.5).then_inc(rough_done, 1)
                if runs_step(k):
                    norm_nodes(uk, R - BY_DVE - 2, R - BY_DVE).then_inc(node_norm_done, 1)
                if ends(i, 0):
                    sigmoid(j)

            steps(act, step, 2, peeled=2)

        @block.vector
        def _(dve):
            nc.vector.memset(index_rows[:, 0:2, :, :], int(PAD))
            nc.vector.memset(index_rows[:, 2, :, :], 0).then_inc(s_pad, 1)
            nc.vector.memset(dst_col[:, 0:1], -1.0).then_inc(s_pad, 1)
            nc.vector.memset(gather_f[:, TILES:, :], 0.0)
            nc.vector.memset(messages[:, :, D:D + 1], 1.0).then_inc(s_ones, 1)
            dve.wait_ge(s_load, 16 * 13)
            dve.wait_ge(s_const, 6)
            chain = [0]

            def link(ins):
                chain[0] += 1
                ins.then_inc(s_prep, 1)
                dve.wait_ge(s_prep, chain[0])

            nc.vector.tensor_copy(limit[:, :], limit_i[:, :])
            link(nc.vector.tensor_copy(index_rows_f[:, :, :, :], index_rows[:, :, :, :]))
            dst_r, next_r = index_rows_f[:, 0, :, :], index_rows_f[:, 1, :, :]
            nc.vector.tensor_tensor(broken[:, :, :], dst_r, next_r, ALU.is_gt)
            link(nc.vector.tensor_scalar(real[:, :, :], dst_r, PAD, None, ALU.is_lt))
            for b in range(2):
                last = nc.vector.scalar_tensor_tensor(out=ahead[:, b, :], in0=dst_r[:, b, :], scalar=limit[:, b:b + 1],
                                                      in1=real[:, b, :], op0=ALU.is_ge, op1=ALU.mult)
            link(nc.vector.tensor_tensor(runs[:, :], dst_r[:, :, 0], dst_r[:, :, P - 1], ALU.is_equal))
            link(nc.vector.tensor_tensor(broken[:, :, :], broken[:, :, :], ahead[:, :, :], ALU.add))
            link(nc.vector.tensor_tensor(runs[:, :], runs[:, :], real[:, :, 0], ALU.mult))
            nc.vector.tensor_reduce(broken_sum[:, :], broken[:, :, :], AX.XY, ALU.add)
            link(nc.vector.tensor_reduce(runs_sum[:, :], runs[:, :], AX.X, ALU.add))
            nc.vector.tensor_tensor(violations[:, :], broken_sum[:, :], runs_sum[:, :], ALU.add).then_inc(s_viol, 1)
            cols = cols_ps[:, :, :].rearrange("p b e -> p (b e)")
            dve.wait_ge(s_cols, 1)
            nc.vector.tensor_copy(dst_col[:, 1:1 + TILES], cols[:, 0:TILES]).then_inc(s_cols_out, 1)
            dve.wait_ge(s_cols_out, 1)
            nc.vector.tensor_scalar(gather_f[:, 0:TILES, 1], dst_col[:, 1:1 + TILES], float(NODES - 1), None, ALU.min)
            dve.wait_ge(s_cols, 2)
            nc.vector.tensor_tensor(next_col[:, :], dst_col[:, 1:1 + TILES], cols[:, 0:TILES], ALU.is_equal).then_inc(s_cols_out, 1)
            dve.wait_ge(s_cols, 3)
            nc.vector.tensor_copy(gather_f[:, 0:TILES, 0], cols[:, 0:TILES]).then_inc(s_cols_out, 1)
            dve.wait_ge(s_cols_out, 3)
            dve.wait_ge(s_viol_ps, 1)
            link(nc.vector.tensor_scalar(skip[:, :], r_ps[:, 0:1], 0.5, None, ALU.is_gt))
            nc.vector.tensor_copy(flag[:, :], skip[:, :]).then_inc(s_flag, 1)
            link(nc.vector.tensor_scalar(next_col[:, :], next_col[:, :], skip[:, 0:1], PAD, ALU.max, ALU.mult))
            link(nc.vector.tensor_tensor(scatter_f[:, :], next_col[:, :], dst_col[:, 1:1 + TILES], ALU.add))

            def gather_columns(i, u):
                cols4 = bass.ds(i * TB, TB) if not isinstance(i, int) else slice(i * TB, (i + 1) * TB)
                nc.vector.tensor_copy(gather_idx[u][:, :, :], gather_f[:, cols4, :]).then_inc(gather_idx_ready, 1)

            for u in range(NS):
                gather_columns(u, u)

            def tiles_of(i, first=0):
                if isinstance(i, int):
                    return slice(i * TB + first, i * TB + first + TB)
                return bass.ds(i * TB + first, TB)

            def node_stats(u, lo, hi):
                for r in range(lo, hi):
                    last = nc.vector.bn_stats(stats[:, 2 * TB + r, :], node_x[u][:, r, :])
                return last

            def counts(m, om, um):
                wait(dve, sum_done, m + 1)
                nc.vector.tensor_scalar(count[:, :], sum_ps[:, :, D], 1.0, None, ALU.max).then_inc(count_done, 1)
                wait(dve, scattered[um], om * (16 * TB))
                nc.vector.tensor_copy(scatter_idx[um][:, :], scatter_f[:, tiles_of(m)])

            def inverse_counts(m):
                wait(dve, count_done, m + 1)
                nc.vector.reciprocal(inv_count[:, :], count[:, :]).then_inc(inv_done, 1)

            def rows_to_write(m, um, lo, hi):
                wait(dve, inv_done, m + 1)
                for t in range(lo, hi):
                    last = nc.vector.scalar_tensor_tensor(out=final[um][:, t, :], in0=sum_ps[:, t, 0:D],
                                                          scalar=inv_count[:, t:t + 1], in1=base[um % 2][:, t, :],
                                                          op0=ALU.mult, op1=ALU.add)
                if hi == TB:
                    last.then_inc(final_done, 1)

            def message(n):
                wait(dve, gate_done, n + 1)
                wait(dve, softplus_done, n + 1)
                nc.vector.tensor_tensor(messages[:, tiles_of(n), 0:D], gate[:, :, :], softplus[:, :, :],
                                        ALU.mult).then_inc(message_done, 1)

            def equality(n, on, un):
                wait(dve, across_loaded[un], on * 16 + 16)
                wait(dve, sum_done, n)
                for prev in range(2):
                    col = dst_col[:, tiles_of(n, 1 - prev)].unsqueeze(2).to_broadcast([P, TB, P])
                    last = nc.vector.tensor_tensor(same[:, prev, :, :], dst_across[un][:, :, :], col, ALU.is_equal)
                last.then_inc(same_done, 1)

            def step(i, o, u):
                k, ok, uk = back(i, o, u, 1)
                j, oj, uj = back(i, o, u, 2)
                m, om, um = back(i, o, u, 3)
                now = runs_step(i)
                edge_turn = runs_step(m) and not ends(i, 1)
                if now:
                    dve.wait_ge(node_loaded[u], o * 16 + 16)
                if runs_step(k):
                    wait(dve, rough_done, k + 1)
                    nc.vector.tensor_tensor(rough_sq[:, :], rough[:, :], rough[:, :], ALU.mult).then_inc(newton1_done, 1)
                    if now:
                        node_stats(u, 0, 1)
                    wait(dve, newton1_done, k + 1)
                    nc.vector.scalar_tensor_tensor(out=correction[:, :], in0=rough_sq[:, :], scalar=-0.5 / D, in1=var96[:, :],
                                                   op0=ALU.mult, op1=ALU.mult).then_inc(newton2_done, 1)
                    if now:
                        node_stats(u, 1, 2)
                    wait(dve, newton2_done, k + 1)
                    wait(dve, node_norm_done, k - NS + 1)
                    nc.vector.scalar_tensor_tensor(out=rstd[uk][:, :], in0=correction[:, :], scalar=1.5, in1=rough[:, :],
                                                   op0=ALU.add, op1=ALU.mult).then_inc(rstd_done, 1)
                    if now:
                        node_stats(u, 2, 3)
                    wait(dve, rstd_done, k + 1)
                    nc.vector.scalar_tensor_tensor(out=shift[uk][:, :], in0=mean2[uk][:, :], scalar=-0.5, in1=rstd[uk][:, :],
                                                   op0=ALU.mult, op1=ALU.mult).then_inc(shift_done, 1)
                elif now:
                    node_stats(u, 0, 3)
                if runs_step(j):
                    wait(dve, final_done, j - 1)
                    wait(dve, edge_norm_done, j + 1)
                    nc.vector.tensor_tensor(base[uj % 2][:, :, :], edge_x[uj][:, :, 1, :], concat[uj][:, :, D:2 * D],
                                            ALU.add).then_inc(base_done, 1)
                    wait(dve, node_norm_done, j + 1)
                    wait(dve, dve_norm_done, j + 1)
                    nc.vector.scalar_tensor_tensor(out=node_out[uj][:, :, :], in0=node_out[uj][:, :, :], scalar=0.0,
                                                   in1=node_x[uj][:, :, :], op0=ALU.max, op1=ALU.add).then_inc(node_sum_done, 1)
                if runs_step(k):
                    wait(dve, shift_done, k + 1)
                    wait(dve, node_stored[uk], ok * 16)
                    for r in range(R - BY_DVE, R):
                        c = 2 * TB + r
                        last = nc.vector.tensor_scalar(node_out[uk][:, r, :], node_x[uk][:, r, :], rstd[uk][:, c:c + 1],
                                                       shift[uk][:, c:c + 1], ALU.mult, ALU.add)
                    last.then_inc(dve_norm_done, 1)
                if edge_turn:
                    equality(m, om, um)
                    message(m)
                if now:
                    node_stats(u, 3, R)
                    dve.wait_ge(gathered[u], o * (16 * 2 * TB) + 16 * 2 * TB)
                    for r in range(2 * TB):
                        last = nc.vector.bn_stats(stats[:, r, :], edge_x[u][:, r // 2, r % 2, :])
                    last.then_inc(stats_done, 1)
                    n = i + NS
                    if not isinstance(n, int) or n < STEPS:
                        gather_columns(n, u)
                if edge_turn:
                    counts(m, om, um)
                if now:
                    wait(dve, stats_done, i + 1)
                    nc.vector.tensor_tensor(half_diff[:, :], stats[:, :, 1], stats[:, :, 4], ALU.subtract).then_inc(parts_done, 1)
                    nc.vector.scalar_tensor_tensor(out=sq_sum[:, :], in0=stats[:, :, 2], scalar=D * EPS, in1=stats[:, :, 5],
                                                   op0=ALU.add, op1=ALU.add).then_inc(parts_done, 1)
                    nc.vector.tensor_tensor(mean2[u][:, :], stats[:, :, 1], stats[:, :, 4], ALU.add).then_inc(parts_done, 1)
                if edge_turn:
                    inverse_counts(m)
                if now:
                    wait(dve, parts_done, i * 3 + 3)
                    nc.vector.tensor_tensor(diff_sq[:, :], half_diff[:, :], half_diff[:, :], ALU.mult).then_inc(diff_sq_done, 1)
                if edge_turn:
                    rows_to_write(m, um, 0, 2)
                if now:
                    wait(dve, diff_sq_done, i + 1)
                    nc.vector.scalar_tensor_tensor(out=var96[:, :], in0=diff_sq[:, :], scalar=D / 4.0, in1=sq_sum[:, :],
                                                   op0=ALU.mult, op1=ALU.add).then_inc(var_done, 1)
                if edge_turn:
                    rows_to_write(m, um, 2, TB)
                if runs_step(j):
                    wait(dve, log1p_done, j + 1)
                    wait(dve, gate_done, j)
                    nc.vector.scalar_tensor_tensor(out=log_gate[:, :, :], in0=z_ps[uj % 2][:, :, 0:D], scalar=0.0,
                                                   in1=log1p[:, :, 0:D], op0=ALU.min, op1=ALU.subtract
                                                   ).then_inc(log_gate_done, 1)
                if runs_step(j):
                    wait(dve, message_done, j)
                    nc.vector.scalar_tensor_tensor(out=softplus[:, :, :], in0=z_ps[uj % 2][:, :, D:2 * D], scalar=0.0,
                                                   in1=log1p[:, :, D:2 * D], op0=ALU.max, op1=ALU.add
                                                   ).then_inc(softplus_done, 1)
                if ends(i, 0):
                    equality(j, oj, uj)
                    message(j)
                    counts(j, oj, uj)
                    inverse_counts(j)
                    rows_to_write(j, uj, 0, TB)

            steps(dve, step, 2, peeled=2)

            bad = dve.value_load(flag[0:1, 0:1], min_val=0, max_val=1)

            def tile_indices(t, n):
                dst_t = dst_col[:, bass.ds(t + 1, 1)]
                dve.wait_ge(r_written, n * 16 + 16)
                nc.vector.tensor_scalar(diag, ident[:, :], dst_t, None, ALU.mult).then_inc(r_diag_done, 1)
                dve.wait_ge(r_across_done, n + 1)
                nc.vector.tensor_scalar(r_same, r_ps[:, P:2 * P], dst_t, None, ALU.is_equal).then_inc(r_same_done, 1)
                dve.wait_ge(r_same_done, n + 1)
                nc.vector.tensor_tensor(r_later, r_same, later[:, :], ALU.mult).then_inc(r_later_done, 1)
                dve.wait_ge(r_sum_done, n + 1)
                nc.vector.tensor_scalar(r_mask[:, :], r_ps[:, D + 1:D + 2], 0.5, PAD, ALU.is_gt, ALU.mult).then_inc(r_mask_done, 1)
                nc.vector.tensor_scalar(r_gather_f[:, :], dst_t, float(NODES - 1), None, ALU.min).then_inc(r_mask_done, 1)
                dve.wait_ge(r_mask_done, n * 2 + 2)
                nc.vector.tensor_copy(r_gather[:, :], r_gather_f[:, :])
                nc.vector.tensor_tensor(r_scatter[:, :], r_mask[:, :], dst_t, ALU.add).then_inc(r_idx_done, 1)

            with dve.If(bad != 0):
                nc.vector.memset(zeros, 0.0).then_inc(r_zeroed, 1)
                with dve.Fori(0, TILES) as t:
                    tile_indices(t, t)
                    dve.wait_ge(r_gathered, t * 16 + 16)
                    nc.vector.tensor_tensor(r_count_new[:, :], r_count[:, :], r_ps[:, D:D + 1], ALU.add).then_inc(r_new_done, 1)
                with dve.Fori(0, TILES) as t:
                    tile_indices(t, t + TILES)
                    dve.wait_ge(r_gathered, t * 32 + 16 * TILES + 32)
                    nc.vector.tensor_scalar(r_count_new[:, :], r_count[:, :], 1.0, None, ALU.max).then_inc(r_clamped, 1)
                    dve.wait_ge(r_clamped, t + 1)
                    nc.vector.reciprocal(r_inv[:, :], r_count_new[:, :]).then_inc(r_inv_done, 1)
                    dve.wait_ge(r_inv_done, t + 1)
                    nc.vector.scalar_tensor_tensor(out=r_row_new[:, :], in0=r_ps[:, 0:D], scalar=r_inv[:, 0:1], in1=r_row[:, :],
                                                   op0=ALU.mult, op1=ALU.add).then_inc(r_new_done, 1)

        @block.tensor
        def _(pe):
            pe.wait_ge(s_const, 6)
            pe.wait_ge(s_prep, 1)
            for n, row in enumerate((0, 1, 2)):
                if n:
                    pe.wait_ge(s_cols_out, n)
                nc.tensor.transpose(cols_ps[:, 0, :], index_rows_f[:, row, 0, :], ident[:, :])
                k = TILES - P
                nc.tensor.transpose(cols_ps[:, 1, 0:k], index_rows_f[0:k, row, 1, :], ident[0:k, 0:k]).then_inc(s_cols, 1)
            pe.wait_ge(s_viol, 1)
            pe.wait_ge(s_cols_out, 3)
            nc.tensor.matmul(r_ps[:, 0:1], ones[:, :], violations[:, :], start=True, stop=True).then_inc(s_viol_ps, 1)
            pe.wait_ge(s_ones, 1)
            pe.wait_ge(s_load, 16 * 13)

            def sums(j):
                wait(pe, message_done, j + 1)
                wait(pe, same_done, j + 1)
                wait(pe, final_done, j)
                for t in range(TB):
                    if isinstance(j, int):
                        cur, prev = messages[:, j * TB + t, :], messages[:, max(j * TB + t - 1, 0), :]
                    else:
                        cur = messages[:, bass.ds(j * TB + t, 1), :].rearrange("p a c -> p (a c)")
                        prev = messages[:, bass.ds(j * TB + (t - 1), 1), :].rearrange("p a c -> p (a c)")
                    nc.tensor.matmul(sum_ps[:, t, :], same[:, 0, t, :], cur, start=True, stop=False)
                    last = nc.tensor.matmul(sum_ps[:, t, :], same[:, 1, t, :], prev, start=False, stop=True)
                last.then_inc(sum_done, 1)

            def step(i, o, u):
                k, ok, uk = back(i, o, u, 1)
                if runs_step(k):
                    wait(pe, edge_norm_done, k + 1)
                    pe.wait_ge(edge_loaded[uk], ok * 16 + (32 if isinstance(k, int) and k == STEPS - 1 else 16))
                    for h in range(2):
                        wait(pe, trans_out[h], k)
                        for t in range(2):
                            for b in range(2):
                                last = nc.tensor.transpose(trans_ps[h][:, t, b, :], concat[uk][:, 2 * h + t, b * P:(b + 1) * P],
                                                           ident[:, :])
                        last.then_inc(trans_done[h], 1)
                m = i - 3
                if runs_step(m) and not ends(i, 1):
                    sums(m)
                if runs_step(k):
                    wait(pe, softplus_done, k - 1)
                    for h in range(2):
                        wait(pe, trans_out[h], k + 1)
                        for t in range(2):
                            z = z_ps[uk % 2][:, 2 * h + t, 0:2 * D]
                            nc.tensor.matmul(z, ones[0:1, :], bias[0:1, :], start=True, stop=False)
                            for b in range(2):
                                last = nc.tensor.matmul(z, concat_t[:, h, t, b, :], weights[:, b, :], start=False, stop=(b == 1))
                    last.then_inc(z_done, 1)
                if ends(i, 0):
                    sums(i - 2)

            steps(pe, step, 2, peeled=2)

            pe.wait_ge(s_flag, 1)
            bad = pe.value_load(flag[0:1, 0:1], min_val=0, max_val=1)

            def tile_sums(t, n):
                pe.wait_ge(r_diag_done, n + 1)
                nc.tensor.matmul(r_ps[:, P:2 * P], ones[:, :], diag, start=True, stop=True).then_inc(r_across_done, 1)
                pe.wait_ge(r_later_done, n + 1)
                m = messages[:, bass.ds(t, 1), :].rearrange("p a c -> p (a c)")
                nc.tensor.matmul(r_ps[:, 0:D + 1], r_same, m, start=True, stop=True)
                nc.tensor.matmul(r_ps[:, D + 1:D + 2], r_later, ones[:, 0:1], start=True, stop=True).then_inc(r_sum_done, 1)

            with pe.If(bad != 0):
                with pe.Fori(0, TILES) as t:
                    tile_sums(t, t)
                with pe.Fori(0, TILES) as t:
                    tile_sums(t, t + TILES)


_INS = ["x", "src", "dst", "edge_attr_64", "L0_gnn_W_e", "L0_gnn_b_e", "L0_gnn_W_n", "L0_gnn_b_n"]


def kernel(**inputs):
    import numpy as _np
    import concourse.bacc as _bacc
    from concourse import mybir as _mybir
    from concourse.bass_utils import run_bass_kernel_spmd as _run

    nc = _bacc.Bacc("TRN2", target_bir_lowering=False, num_devices=1)
    arrays, args = {}, []
    for name in _INS:
        a = _np.ascontiguousarray(inputs[name])
        arrays[f"in_{name}"] = a
        args.append(nc.dram_tensor(f"in_{name}", a.shape, _mybir.dt.from_np(a.dtype), kind="ExternalInput").ap())
    out = nc.dram_tensor("out", (NODES, D), FP32, kind="ExternalOutput").ap()
    count_table = nc.dram_tensor("count_table", (NODES, 1), FP32, kind="Internal").ap()
    build(nc, *args, out, count_table)
    return _run(nc, [arrays], core_ids=[0]).results[0]["out"]
```

```python
import concourse.bass as bass
from concourse import mybir
from contextlib import ExitStack

FP32 = mybir.dt.float32
I32 = mybir.dt.int32
ALU = mybir.AluOpType
ACT = mybir.ActivationFunctionType
AX = mybir.AxisListType

P = 128
NODES, D = 100000, 96
EDGES, DE = 25000, 64
IN = 2 * D + DE
TILES = -(-EDGES // P)
TB = 4
STEPS = TILES // TB
LAST_EDGES = EDGES - (TILES - 1) * P
R = 16
CHUNK = P * R
ROWS = 2 * TB + R
NS = 4
OUTER = (STEPS - 1) // NS
BY_DVE = 2
PAD = float(1 << 20)
LEAD = 2
AHEAD = 2
EPS = 1e-5
SLACK = AHEAD * CHUNK - (TB - 1) * (CHUNK // TB)
assert STEPS * TB == TILES and OUTER * NS + 1 == STEPS and STEPS * CHUNK >= NODES > (STEPS - 1) * CHUNK


def build(nc, x, src, dst, edge_attr, w_e, b_e, w_n, b_n, out, count_table):
    ctx = ExitStack()
    with ctx:
        def sb(name, shape, dt=FP32):
            return ctx.enter_context(nc.sbuf_tensor(name, shape, dt))

        def pb(name, shape):
            return ctx.enter_context(nc.psum_tensor(name, shape, FP32))

        def sem(name):
            return ctx.enter_context(nc.semaphore(name))

        def sems(name):
            return [sem(f"{name}{u}") for u in range(NS)]

        ident = sb("ident", [P, P])
        ones = sb("ones", [P, P])
        later = sb("later", [P, P])
        weights = sb("weights", [P, 2, 2 * D])
        bias = sb("bias", [1, 2 * D])
        index_rows = sb("index_rows", [P, 3, 2, P], I32)
        index_rows_f = sb("index_rows_f", [P, 3, 2, P])
        limit_i = sb("limit_i", [P, 2], I32)
        limit = sb("limit", [P, 2])
        real = sb("real", [P, 2, P])
        broken = sb("broken", [P, 2, P])
        ahead = sb("ahead", [P, 2, P])
        runs = sb("runs", [P, 2])
        broken_sum = sb("broken_sum", [P, 1])
        runs_sum = sb("runs_sum", [P, 1])
        violations = sb("violations", [P, 1])
        skip = sb("skip", [P, 1])
        flag = sb("flag", [P, 1], I32)
        dst_col = sb("dst_col", [P, 1 + TILES])
        next_col = sb("next_col", [P, TILES])
        gather_f = sb("gather_f", [P, TILES + (NS - 1) * TB, 2])
        scatter_f = sb("scatter_f", [P, TILES])
        gather_idx = [sb(f"gather_idx{u}", [P, TB, 2], I32) for u in range(NS)]
        scatter_idx = [sb(f"scatter_idx{u}", [P, TB], I32) for u in range(NS)]
        node_x = [sb(f"node_x{u}", [P, R, D]) for u in range(NS)]
        node_out = [sb(f"node_out{u}", [P, R, D]) for u in range(NS)]
        edge_x = [sb(f"edge_x{u}", [P, TB, 2, D]) for u in range(NS)]
        concat = [sb(f"concat{u}", [P, TB, IN]) for u in range(NS)]
        dst_across = [sb(f"dst_across{u}", [P, TB, P], I32) for u in range(NS)]
        base = [sb(f"base{u}", [P, TB, D]) for u in range(2)]
        for b in range(2):
            room = index_rows_f[:, :, :, :].rearrange("p a b e -> p (a b e)")[:, b * TB * D:(b + 1) * TB * D]
            base.append(room.rearrange("p (t d) -> p t d", t=TB))
        final = [sb(f"final{u}", [P, TB, D]) for u in range(NS)]
        rstd = [sb(f"rstd{u}", [P, ROWS]) for u in range(NS)]
        shift = [sb(f"shift{u}", [P, ROWS]) for u in range(NS)]
        stats = sb("stats", [P, ROWS, 6])
        half_diff = sb("half_diff", [P, ROWS])
        mean2 = [sb(f"mean2_{u}", [P, ROWS]) for u in range(NS)]
        sq_sum = sb("sq_sum", [P, ROWS])
        diff_sq = sb("diff_sq", [P, ROWS])
        var96 = sb("var96", [P, ROWS])
        log_var = sb("log_var", [P, ROWS])
        rough = sb("rough", [P, ROWS])
        rough_sq = sb("rough_sq", [P, ROWS])
        correction = sb("correction", [P, ROWS])
        concat_t = sb("concat_t", [P, 2, 2, 2, P])
        magnitude = sb("magnitude", [P, TB, 2 * D])
        log1p = sb("log1p", [P, TB, 2 * D])
        log_gate = sb("log_gate", [P, TB, D])
        gate = sb("gate", [P, TB, D])
        softplus = sb("softplus", [P, TB, D])
        same = sb("same", [P, 2, TB, P])
        count = sb("count", [P, TB])
        inv_count = sb("inv_count", [P, TB])
        messages = sb("messages", [P, TILES, D + 1])
        zeros = node_x[0][0:80, :, :].rearrange("p r d -> p (r d)")[:, 0:NODES // 80]
        diag = same[:, 0, 0, :]
        r_same = same[:, 0, 1, :]
        r_later = same[:, 0, 2, :]
        r_gather = sb("r_gather", [P, 1], I32)
        r_scatter = sb("r_scatter", [P, 1], I32)
        r_gather_f = sb("r_gather_f", [P, 1])
        r_mask = sb("r_mask", [P, 1])
        r_count = sb("r_count", [P, 1])
        r_count_new = sb("r_count_new", [P, 1])
        r_inv = sb("r_inv", [P, 1])
        r_row = sb("r_row", [P, D])
        r_row_new = sb("r_row_new", [P, D])

        trans_ps = [pb(f"trans_ps{h}", [P, 2, 2, P]) for h in range(2)]
        z_ps = [pb(f"z_ps{v}", [P, TB, 256]) for v in range(2)]
        sum_ps = pb("sum_ps", [P, TB, D + 1])
        side_ps = pb("side_ps", [P, 512])
        cols_ps = [side_ps[:, 0:2 * P], trans_ps[0][:, 0, :, :].rearrange("p b e -> p (b e)"),
                   trans_ps[1][:, 0, :, :].rearrange("p b e -> p (b e)")]
        r_ps = side_ps[:, 2 * P:4 * P]

        const_done = sem("const_done")
        padding_done = sem("padding_done")
        dst_rows_loaded = sem("dst_rows_loaded")
        src_rows_loaded = sem("src_rows_loaded")
        next_rows_loaded = sem("next_rows_loaded")
        weights_loaded = sem("weights_loaded")
        rows_f_done = sem("rows_f_done")
        cols_done = sem("cols_done")
        cols_read = sem("cols_read")
        gather_f_done = sem("gather_f_done")
        check_done = sem("check_done")
        violations_done = sem("violations_done")
        violations_summed = sem("violations_summed")
        flag_done = sem("flag_done")
        message_ones_done = sem("message_ones_done")
        node_loaded = sems("node_loaded")
        edge_loaded = sems("edge_loaded")
        across_loaded = sems("across_loaded")
        gathered = sems("gathered")
        node_stored = sems("node_stored")
        scattered = sems("scattered")
        gather_idx_ready = sem("gather_idx_ready")
        stats_done = sem("stats_done")
        parts_done = sem("parts_done")
        diff_sq_done = sem("diff_sq_done")
        var_done = sem("var_done")
        log_var_done = sem("log_var_done")
        rough_done = sem("rough_done")
        newton1_done = sem("newton1_done")
        newton2_done = sem("newton2_done")
        rstd_done = sem("rstd_done")
        shift_done = sem("shift_done")
        edge_norm_done = sem("edge_norm_done")
        dve_norm_done = sem("dve_norm_done")
        node_norm_done = sem("node_norm_done")
        base_done = sem("base_done")
        node_sum_done = sem("node_sum_done")
        trans_done = [sem(f"trans_done{h}") for h in range(2)]
        trans_out = [sem(f"trans_out{h}") for h in range(2)]
        z_done = sem("z_done")
        magnitude_done = sem("magnitude_done")
        decay_done = sem("decay_done")
        log1p_done = sem("log1p_done")
        log_gate_done = sem("log_gate_done")
        softplus_done = sem("softplus_done")
        gate_done = sem("gate_done")
        message_done = sem("message_done")
        same_done = sem("same_done")
        sum_done = sem("sum_done")
        count_done = sem("count_done")
        inv_done = sem("inv_done")
        final_done = sem("final_done")
        pool_go = sem("pool_go")
        r_zeroed = sem("r_zeroed")
        r_written = sem("r_written")
        r_diag_done = sem("r_diag_done")
        r_across_done = sem("r_across_done")
        r_same_done = sem("r_same_done")
        r_later_done = sem("r_later_done")
        r_sum_done = sem("r_sum_done")
        r_mask_done = sem("r_mask_done")
        r_idx_done = sem("r_idx_done")
        r_gathered = sem("r_gathered")
        r_clamped = sem("r_clamped")
        r_inv_done = sem("r_inv_done")
        r_new_done = sem("r_new_done")

        block = ctx.enter_context(nc.Block())

        def steps(eng, step, tail, peeled=2, until=OUTER):
            for i in range(NS * peeled):
                step(i, i // NS, i % NS)
            with eng.Fori(peeled, until) as o:
                for u in range(NS):
                    step(o * NS + u, o, u)
            for i in range(until * NS, STEPS + tail):
                step(i, i // NS, i % NS)

        def back(i, o, u, n):
            return i - n, o - (1 if n % NS > u else 0) - n // NS, (u - n) % NS

        def runs_step(i):
            return not isinstance(i, int) or 0 <= i < STEPS

        def runs_rows(i):
            return not isinstance(i, int) or -LEAD <= i < STEPS

        def last_rows(i):
            return isinstance(i, int) and i == STEPS - 1

        def first_steps(step):
            for i in range(-LEAD, 0):
                step(i, i // NS, i % NS)

        def ends(i, passed):
            return isinstance(i, int) and i >= STEPS + passed and i - 2 < STEPS

        def wait(eng, semaphore, value):
            if not isinstance(value, int) or value > 0:
                eng.wait_ge(semaphore, value)

        def chunk_of(t, i):
            if isinstance(i, int):
                first = min(i * CHUNK, NODES - CHUNK)
                return t[first:first + CHUNK, :].rearrange("(p r) d -> p r d", p=P)
            v = t[0:(STEPS - 1) * CHUNK, :].rearrange("(c p r) d -> c p r d", p=P, r=R)
            return v[bass.ds(i, 1), :, :, :].rearrange("a p r d -> (a p) r d")

        def load_index_rows(eng, n, t, shift_by, loaded):
            half = P * P
            full = (TILES - 1) * P
            k = LAST_EDGES - shift_by
            eng.dma_start(index_rows[:, n, 0, :], t[shift_by:shift_by + half].rearrange("(t e) -> t e", e=P)).then_inc(loaded, 16)
            eng.wait_ge(padding_done, 1)
            eng.dma_start(index_rows[0:TILES - 1 - P, n, 1, :],
                          t[half + shift_by:full + shift_by].rearrange("(t e) -> t e", e=P)).then_inc(loaded, 16)
            eng.dma_start(index_rows[TILES - 1 - P:TILES - P, n, 1, 0:k],
                          t[full + shift_by:EDGES].rearrange("(a e) -> a e", a=1)).then_inc(loaded, 16)

        @block.sync
        def _(sp):
            load_index_rows(sp, 0, dst, 0, dst_rows_loaded)

            def step(i, o, u):
                n, on, un = back(i, o, u, LEAD)
                tail = (STEPS - 1) * TB * P
                if runs_step(n):
                    wait(sp, trans_done[1], n - NS + 1)
                    if isinstance(n, int) and n == STEPS - 1:
                        m = (TB - 1) * P
                        sp.dma_start(concat[un][:, 0:TB - 1, 2 * D:IN],
                                     edge_attr[tail:tail + m, :].rearrange("(t p) f -> p t f", p=P)).then_inc(edge_loaded[un], 16)
                        sp.dma_start(concat[un][0:LAST_EDGES, TB - 1, 2 * D:IN],
                                     edge_attr[tail + m:EDGES, :]).then_inc(edge_loaded[un], 16)
                    else:
                        ev = edge_attr[0:tail, :].rearrange("(b t p) f -> b p t f", t=TB, p=P)
                        e_src = ev[n, :, :, :] if isinstance(n, int) else ev[bass.ds(n, 1), :, :, :].rearrange("a p t f -> (a p) t f")
                        sp.dma_start(concat[un][:, :, 2 * D:IN], e_src).then_inc(edge_loaded[un], 16)
                j, oj, uj = back(i, o, u, NS)
                if runs_step(j):
                    wait(sp, node_sum_done, j + 1)
                if runs_step(i):
                    sp.dma_start(node_x[u][:, :, :], chunk_of(x, i)).then_inc(node_loaded[u], 16)
                if runs_step(j):
                    if isinstance(j, int) and j == STEPS - 1:
                        sp.wait_ge(node_stored[(j - 1) % NS], 16 * ((j - 1) // NS + 1))
                    sp.dma_start(chunk_of(out, j), node_out[uj][:, :, :]).then_inc(node_stored[uj], 16)
                if isinstance(i, int) and i == 0:
                    load_index_rows(sp, 2, dst, 1, next_rows_loaded)
                k, ok, uk = back(i, o, u, LEAD + 1)
                if runs_step(k):
                    wait(sp, same_done, k - NS + 1)
                    across = dst_across[uk][:, :, :].rearrange("p t e -> p (t e)")
                    dv = dst[0:tail].rearrange("(b e) -> b e", e=TB * P)
                    if isinstance(k, int) and k == STEPS - 1:
                        d_src, across = dst[tail:EDGES], across[:, 0:EDGES - tail]
                    else:
                        d_src = dv[k, :] if isinstance(k, int) else dv[bass.ds(k, 1), :].rearrange("a e -> (a e)")
                    sp.dma_start(across, d_src.partition_broadcast(P)).then_inc(across_loaded[uk], 16)

            steps(sp, step, NS)
            for u in range(NS):
                sp.wait_ge(node_stored[u], 16 * ((STEPS - 1 - u) // NS + 1))

        @block.gpsimd
        def _(pool):
            nc.gpsimd.memset(ident[:, :], 0.0).then_inc(const_done, 1)
            nc.gpsimd.memset(ones[:, :], 1.0).then_inc(const_done, 1)
            for b in range(2):
                nc.gpsimd.iota(limit_i[:, b:b + 1], pattern=[[0, 1]], base=(CHUNK // TB) * P * b + SLACK,
                               channel_multiplier=CHUNK // TB).then_inc(const_done, 1)
            pool.wait_ge(const_done, 4)
            nc.gpsimd.affine_select(out=ident[:, :], in_=ident[:, :], compare_op=ALU.not_equal, fill=1.0, base=0,
                                    pattern=[[-1, P]], channel_multiplier=1).then_inc(const_done, 1)
            nc.gpsimd.affine_select(out=later[:, :], in_=ones[:, :], compare_op=ALU.is_gt, fill=0.0, base=0,
                                    pattern=[[-1, P]], channel_multiplier=1).then_inc(const_done, 1)

            def step(i, o, u):
                if runs_step(i):
                    wait(pool, gather_idx_ready, i + 1)
                    wait(pool, base_done, i - NS + 1)
                    pool.sem_inc(pool_go, 1)
                    for t in range(TB):
                        for side in range(2):
                            nc.gpsimd.indirect_dma_start(
                                out=edge_x[u][:, t, side, :], out_offset=None, in_=x,
                                in_offset=bass.IndirectOffsetOnAxis(ap=gather_idx[u][:, t, side:side + 1], axis=0),
                            ).then_inc(gathered[u], 16)
                lag = NS + 2
                j, oj, uj = back(i, o, u, lag)
                if runs_step(j):
                    wait(pool, final_done, j + 1)
                    for n in range(AHEAD + 1 if isinstance(j, int) and j == 0 else 1):
                        c, oc, uc = back(i, o, u, lag - AHEAD + n)
                        if runs_step(c):
                            pool.wait_ge(node_stored[uc], oc * 16 + 16)
                    pool.sem_inc(pool_go, 1)
                    for t in range(TB):
                        nc.gpsimd.indirect_dma_start(
                            out=out, in_=final[uj][:, t, :], in_offset=None,
                            out_offset=bass.IndirectOffsetOnAxis(ap=scatter_idx[uj][:, t:t + 1], axis=0),
                            bounds_check=NODES - 1, oob_is_err=False).then_inc(scattered[uj], 16)

            steps(pool, step, NS + 2)
            for u in range(NS):
                pool.wait_ge(scattered[u], 16 * TB * ((STEPS - 1 - u) // NS + 1))

            pool.wait_ge(flag_done, 1)
            bad = pool.value_load(flag[0:1, 0:1], min_val=0, max_val=1)
            with pool.If(bad != 0):
                pool.wait_ge(r_zeroed, 1)
                pool.dma_start(count_table.rearrange("(p n) a -> p (n a)", p=80), zeros).then_inc(r_written, 16)
                with pool.Fori(0, TILES) as t:
                    pool.wait_ge(r_idx_done, t + 1)
                    pool.sem_inc(pool_go, 1)
                    nc.gpsimd.indirect_dma_start(out=r_count[:, :], out_offset=None, in_=count_table,
                                                 in_offset=bass.IndirectOffsetOnAxis(ap=r_gather[:, :], axis=0)
                                                 ).then_inc(r_gathered, 16)
                    pool.wait_ge(r_new_done, t + 1)
                    pool.sem_inc(pool_go, 1)
                    nc.gpsimd.indirect_dma_start(out=count_table, in_=r_count_new[:, :], in_offset=None,
                                                 out_offset=bass.IndirectOffsetOnAxis(ap=r_scatter[:, :], axis=0),
                                                 bounds_check=NODES - 1, oob_is_err=False).then_inc(r_written, 16)
                    pool.wait_ge(r_written, t * 16 + 32)
                with pool.Fori(0, TILES) as t:
                    pool.wait_ge(r_idx_done, t + TILES + 1)
                    pool.sem_inc(pool_go, 1)
                    nc.gpsimd.indirect_dma_start(out=r_count[:, :], out_offset=None, in_=count_table,
                                                 in_offset=bass.IndirectOffsetOnAxis(ap=r_gather[:, :], axis=0)
                                                 ).then_inc(r_gathered, 16)
                    nc.gpsimd.indirect_dma_start(out=r_row[:, :], out_offset=None, in_=out,
                                                 in_offset=bass.IndirectOffsetOnAxis(ap=r_gather[:, :], axis=0)
                                                 ).then_inc(r_gathered, 16)
                    pool.wait_ge(r_new_done, t + TILES + 1)
                    pool.sem_inc(pool_go, 1)
                    nc.gpsimd.indirect_dma_start(out=out, in_=r_row_new[:, :], in_offset=None,
                                                 out_offset=bass.IndirectOffsetOnAxis(ap=r_scatter[:, :], axis=0),
                                                 bounds_check=NODES - 1, oob_is_err=False).then_inc(r_written, 16)
                    pool.wait_ge(r_written, t * 16 + 16 * TILES + 32)

        @block.scalar
        def _(act):
            load_index_rows(act, 1, src, 0, src_rows_loaded)
            for n, w in enumerate((w_e, w_n)):
                act.dma_start(weights[:, :, n * D:(n + 1) * D], w.rearrange("(b p) d -> p b d", p=P)).then_inc(weights_loaded, 16)
            for n, b in enumerate((b_e, b_n)):
                act.dma_start(bias[:, n * D:(n + 1) * D], b.rearrange("(a d) -> a d", a=1)).then_inc(weights_loaded, 16)

            nc.scalar.preload_act_table_set("natural_log_exp_and_others")

            def norm_nodes(u, us, lo, hi):
                for r in range(lo, hi):
                    c = 2 * TB + r
                    last = nc.scalar.activation(node_out[u][:, r, :], node_x[u][:, r, :], ACT.Relu,
                                                bias=shift[us][:, c:c + 1], scale=rstd[us][:, c:c + 1])
                return last

            def log_of_var(i):
                wait(act, var_done, i + 1 + LEAD)
                nc.scalar.activation(log_var[:, :], var96[:, :], ACT.Ln, scale=1.0 / D).then_inc(log_var_done, 1)

            def first_guess(i):
                wait(act, log_var_done, i + 1 + LEAD)
                nc.scalar.activation(rough[:, :], log_var[:, :], ACT.Exp, scale=-0.5).then_inc(rough_done, 1)

            def sigmoid(n):
                wait(act, log_gate_done, n + 1)
                wait(act, message_done, n)
                nc.scalar.activation(gate[:, :, :], log_gate[:, :, :], ACT.Exp).then_inc(gate_done, 1)

            def step(i, o, u):
                k, ok, uk = back(i, o, u, 1)
                j, oj, uj = back(i, o, u, 2)
                m, om, um = back(i, o, u, 3)
                n, on, un = back(i, o, u, 1 - LEAD)
                if runs_step(m) and not ends(i, 1):
                    sigmoid(m)
                if runs_rows(k):
                    wait(act, shift_done, k + 1 + LEAD)
                if runs_step(k):
                    wait(act, trans_done[1], k - NS + 1)
                    wait(act, base_done, k - NS + 1)
                    for t in range(TB):
                        for side in range(2):
                            c = 2 * t + side
                            last = nc.scalar.activation(concat[uk][:, t, side * D:(side + 1) * D], edge_x[uk][:, t, side, :],
                                                        ACT.Relu, bias=shift[uk][:, c:c + 1], scale=rstd[uk][:, c:c + 1])
                    last.then_inc(edge_norm_done, 1)
                if runs_step(n):
                    wait(act, node_stored[un], on * 16)
                    norm_nodes(un, uk, 0, 4)
                for h in range(2):
                    if runs_step(k):
                        wait(act, trans_done[h], k + 1)
                        wait(act, z_done, k)
                        nc.scalar.activation(concat_t[:, h, :, :, :], trans_ps[h][:, :, :, :], ACT.Copy).then_inc(trans_out[h], 1)
                    if h == 0 and runs_step(n):
                        norm_nodes(un, uk, 4, 5)
                if last_rows(i):
                    log_of_var(i)
                    first_guess(i)
                if runs_step(j):
                    wait(act, z_done, j + 1)
                    wait(act, log1p_done, j)
                    nc.scalar.activation(magnitude[:, :, :], z_ps[uj % 2][:, :, 0:2 * D], ACT.Abs).then_inc(magnitude_done, 1)
                if runs_step(n):
                    norm_nodes(un, uk, 5, 6)
                if runs_step(j):
                    wait(act, magnitude_done, j + 1)
                    nc.scalar.activation(magnitude[:, :, :], magnitude[:, :, :], ACT.Exp, scale=-1.0).then_inc(decay_done, 1)
                if runs_step(n):
                    norm_nodes(un, uk, 6, 7)
                if runs_step(j):
                    wait(act, decay_done, j + 1)
                    wait(act, softplus_done, j)
                    nc.scalar.activation(log1p[:, :, :], magnitude[:, :, :], ACT.Ln, bias=1.0).then_inc(log1p_done, 1)
                if runs_step(n):
                    norm_nodes(un, uk, 7, R - BY_DVE - 4)
                if runs_rows(i) and not last_rows(i):
                    log_of_var(i)
                if runs_step(n):
                    norm_nodes(un, uk, R - BY_DVE - 4, R - BY_DVE - 3)
                if runs_rows(i) and not last_rows(i):
                    first_guess(i)
                if runs_step(n):
                    norm_nodes(un, uk, R - BY_DVE - 3, R - BY_DVE).then_inc(node_norm_done, 1)
                if ends(i, 0):
                    sigmoid(j)

            first_steps(step)
            steps(act, step, 2)

        @block.vector
        def _(dve):
            nc.vector.memset(index_rows[:, 0:3:2, 1, :], int(PAD))
            nc.vector.memset(index_rows[:, 1, 1, :], 0).then_inc(padding_done, 1)
            nc.vector.memset(dst_col[:, 0:1], -1.0).then_inc(padding_done, 1)
            nc.vector.memset(gather_f[:, TILES:, :], 0.0).then_inc(padding_done, 1)
            nc.vector.memset(stats[:, 0:2 * TB, :], 1.0).then_inc(padding_done, 1)
            nc.vector.memset(messages[:, :, D:D + 1], 1.0).then_inc(message_ones_done, 1)
            dve.wait_ge(dst_rows_loaded, 48)
            nc.vector.tensor_copy(index_rows_f[:, 0, :, :], index_rows[:, 0, :, :]).then_inc(rows_f_done, 1)
            dve.wait_ge(src_rows_loaded, 48)
            nc.vector.tensor_copy(index_rows_f[:, 1, :, :], index_rows[:, 1, :, :]).then_inc(rows_f_done, 1)
            dve.wait_ge(cols_done, 1)
            nc.vector.tensor_scalar(gather_f[:, 0:TILES, 1], cols_ps[0][:, 0:TILES], float(NODES - 1), None,
                                    ALU.min).then_inc(gather_f_done, 1)
            dve.wait_ge(cols_done, 2)
            nc.vector.tensor_copy(gather_f[:, 0:TILES, 0], cols_ps[1][:, 0:TILES]).then_inc(gather_f_done, 1)
            dve.wait_ge(padding_done, 4)
            dve.wait_ge(gather_f_done, 2)

            def gather_columns(i, u):
                cols4 = bass.ds(i * TB, TB) if not isinstance(i, int) else slice(i * TB, (i + 1) * TB)
                nc.vector.tensor_copy(gather_idx[u][:, :, :], gather_f[:, cols4, :]).then_inc(gather_idx_ready, 1)

            for u in range(NS):
                gather_columns(u, u)

            links = [0]

            def link(ins):
                links[0] += 1
                ins.then_inc(check_done, 1)
                dve.wait_ge(check_done, links[0])

            def columns_of_dst():
                dve.wait_ge(next_rows_loaded, 48)
                nc.vector.tensor_copy(index_rows_f[:, 2, :, :], index_rows[:, 2, :, :]).then_inc(rows_f_done, 1)
                nc.vector.tensor_copy(dst_col[:, 1:1 + TILES], cols_ps[0][:, 0:TILES]).then_inc(cols_read, 1)
                dve.wait_ge(const_done, 6)
                link(nc.vector.tensor_copy(limit[:, :], limit_i[:, :]))
                dve.wait_ge(cols_read, 1)
                dve.wait_ge(cols_done, 3)
                nc.vector.tensor_tensor(next_col[:, :], dst_col[:, 1:1 + TILES], cols_ps[2][:, 0:TILES],
                                        ALU.is_equal).then_inc(cols_read, 1)

            dst_r, next_r = index_rows_f[:, 0, :, :], index_rows_f[:, 2, :, :]

            def check_order():
                dve.wait_ge(rows_f_done, 3)
                nc.vector.tensor_tensor(broken[:, :, :], dst_r, next_r, ALU.is_gt)
                link(nc.vector.tensor_scalar(real[:, :, :], dst_r, PAD, None, ALU.is_lt))
                for b in range(2):
                    nc.vector.scalar_tensor_tensor(out=ahead[:, b, :], in0=dst_r[:, b, :], scalar=limit[:, b:b + 1],
                                                   in1=real[:, b, :], op0=ALU.is_ge, op1=ALU.mult)
                link(nc.vector.tensor_tensor(runs[:, :], dst_r[:, :, 0], dst_r[:, :, P - 1], ALU.is_equal))

            def sum_violations():
                nc.vector.tensor_tensor(broken[:, :, :], broken[:, :, :], ahead[:, :, :], ALU.add)
                link(nc.vector.tensor_tensor(runs[:, :], runs[:, :], real[:, :, 0], ALU.mult))
                nc.vector.tensor_reduce(broken_sum[:, :], broken[:, :, :], AX.XY, ALU.add)
                link(nc.vector.tensor_reduce(runs_sum[:, :], runs[:, :], AX.X, ALU.add))
                nc.vector.tensor_tensor(violations[:, :], broken_sum[:, :], runs_sum[:, :], ALU.add).then_inc(violations_done, 1)

            def scatter_columns():
                dve.wait_ge(violations_summed, 1)
                link(nc.vector.tensor_scalar(skip[:, :], r_ps[:, 0:1], 0.5, None, ALU.is_gt))
                nc.vector.tensor_copy(flag[:, :], skip[:, :]).then_inc(flag_done, 1)
                dve.wait_ge(cols_read, 2)
                link(nc.vector.tensor_scalar(next_col[:, :], next_col[:, :], skip[:, 0:1], PAD, ALU.max, ALU.mult))
                link(nc.vector.tensor_tensor(scatter_f[:, :], next_col[:, :], dst_col[:, 1:1 + TILES], ALU.add))

            between_steps = {-LEAD: columns_of_dst, 0: check_order, 1: sum_violations, 2: scatter_columns}

            def tiles_of(i, first=0):
                if isinstance(i, int):
                    return slice(i * TB + first, i * TB + first + TB)
                return bass.ds(i * TB + first, TB)

            def node_stats(u, lo, hi):
                for r in range(lo, hi):
                    last = nc.vector.bn_stats(stats[:, 2 * TB + r, :], node_x[u][:, r, :])
                return last

            def counts(m, om, um):
                wait(dve, sum_done, m + 1)
                nc.vector.tensor_scalar(count[:, :], sum_ps[:, :, D], 1.0, None, ALU.max).then_inc(count_done, 1)
                wait(dve, scattered[um], om * (16 * TB))
                nc.vector.tensor_copy(scatter_idx[um][:, :], scatter_f[:, tiles_of(m)])

            def inverse_counts(m):
                wait(dve, count_done, m + 1)
                nc.vector.reciprocal(inv_count[:, :], count[:, :]).then_inc(inv_done, 1)

            def rows_to_write(m, um, lo, hi):
                wait(dve, inv_done, m + 1)
                for t in range(lo, hi):
                    last = nc.vector.scalar_tensor_tensor(out=final[um][:, t, :], in0=sum_ps[:, t, 0:D],
                                                          scalar=inv_count[:, t:t + 1], in1=base[um][:, t, :],
                                                          op0=ALU.mult, op1=ALU.add)
                if hi == TB:
                    last.then_inc(final_done, 1)

            def message(n):
                wait(dve, gate_done, n + 1)
                wait(dve, softplus_done, n + 1)
                nc.vector.tensor_tensor(messages[:, tiles_of(n), 0:D], gate[:, :, :], softplus[:, :, :],
                                        ALU.mult).then_inc(message_done, 1)

            def equality(n, on, un):
                wait(dve, across_loaded[un], on * 16 + 16)
                wait(dve, sum_done, n)
                for prev in range(2):
                    col = dst_col[:, tiles_of(n, 1 - prev)].unsqueeze(2).to_broadcast([P, TB, P])
                    last = nc.vector.tensor_tensor(same[:, prev, :, :], dst_across[un][:, :, :], col, ALU.is_equal)
                last.then_inc(same_done, 1)

            def newton(k, uk, chunk):
                wait(dve, rough_done, k + 1 + LEAD)
                nc.vector.tensor_tensor(rough_sq[:, :], rough[:, :], rough[:, :], ALU.mult).then_inc(newton1_done, 1)
                if chunk is not None:
                    node_stats(chunk, 0, 1)
                wait(dve, newton1_done, k + 1 + LEAD)
                nc.vector.scalar_tensor_tensor(out=correction[:, :], in0=rough_sq[:, :], scalar=-0.5 / D, in1=var96[:, :],
                                               op0=ALU.mult, op1=ALU.mult).then_inc(newton2_done, 1)
                if chunk is not None:
                    node_stats(chunk, 1, 2)
                wait(dve, newton2_done, k + 1 + LEAD)
                wait(dve, node_norm_done, k - NS + 1 + LEAD)
                nc.vector.scalar_tensor_tensor(out=rstd[uk][:, :], in0=correction[:, :], scalar=1.5, in1=rough[:, :],
                                               op0=ALU.add, op1=ALU.mult).then_inc(rstd_done, 1)
                if chunk is not None:
                    node_stats(chunk, 2, 3)
                wait(dve, rstd_done, k + 1 + LEAD)
                nc.vector.scalar_tensor_tensor(out=shift[uk][:, :], in0=mean2[uk][:, :], scalar=-0.5, in1=rstd[uk][:, :],
                                               op0=ALU.mult, op1=ALU.mult).then_inc(shift_done, 1)

            def step(i, o, u):
                k, ok, uk = back(i, o, u, 1)
                j, oj, uj = back(i, o, u, 2)
                m, om, um = back(i, o, u, 3)
                c, oc, uc = back(i, o, u, -LEAD)
                n, on, un = back(i, o, u, 1 - LEAD)
                d, od, ud = back(i, o, u, 2 - LEAD)
                now = runs_step(c)
                edge_turn = runs_step(m) and not ends(i, 1)
                if now:
                    dve.wait_ge(node_loaded[uc], oc * 16 + 16)
                if runs_rows(k) and not last_rows(k):
                    newton(k, uk, uc if now else None)
                elif now:
                    node_stats(uc, 0, 3)
                if runs_step(d):
                    wait(dve, node_norm_done, d + 1)
                    wait(dve, dve_norm_done, d + 1)
                    nc.vector.scalar_tensor_tensor(out=node_out[ud][:, :, :], in0=node_out[ud][:, :, :], scalar=0.0,
                                                   in1=node_x[ud][:, :, :], op0=ALU.max, op1=ALU.add).then_inc(node_sum_done, 1)
                if runs_step(n):
                    wait(dve, shift_done, k + 1 + LEAD)
                    wait(dve, node_stored[un], on * 16)
                    for r in range(R - BY_DVE, R):
                        s = 2 * TB + r
                        last = nc.vector.tensor_scalar(node_out[un][:, r, :], node_x[un][:, r, :], rstd[uk][:, s:s + 1],
                                                       shift[uk][:, s:s + 1], ALU.mult, ALU.add)
                    last.then_inc(dve_norm_done, 1)
                if edge_turn:
                    equality(m, om, um)
                    message(m)
                if now:
                    last = node_stats(uc, 3, R)
                if runs_step(k):
                    wait(dve, final_done, k - NS + 1)
                    wait(dve, edge_norm_done, k + 1)
                    nc.vector.tensor_tensor(base[uk][:, :, :], edge_x[uk][:, :, 1, :], concat[uk][:, :, D:2 * D],
                                            ALU.add).then_inc(base_done, 1)
                if runs_step(i):
                    dve.wait_ge(gathered[u], o * (16 * 2 * TB) + 16 * 2 * TB)
                    for r in range(2 * TB):
                        last = nc.vector.bn_stats(stats[:, r, :], edge_x[u][:, r // 2, r % 2, :])
                if runs_rows(i):
                    last.then_inc(stats_done, 1)
                if runs_step(i) and (not isinstance(i, int) or i + NS < STEPS):
                    gather_columns(i + NS, u)
                if edge_turn and not last_rows(i):
                    counts(m, om, um)
                if runs_rows(i):
                    wait(dve, stats_done, i + 1 + LEAD)
                    nc.vector.tensor_tensor(half_diff[:, :], stats[:, :, 1], stats[:, :, 4], ALU.subtract).then_inc(parts_done, 1)
                    nc.vector.scalar_tensor_tensor(out=sq_sum[:, :], in0=stats[:, :, 2], scalar=D * EPS, in1=stats[:, :, 5],
                                                   op0=ALU.add, op1=ALU.add).then_inc(parts_done, 1)
                    nc.vector.tensor_tensor(mean2[u][:, :], stats[:, :, 1], stats[:, :, 4], ALU.add).then_inc(parts_done, 1)
                if edge_turn and not last_rows(i):
                    inverse_counts(m)
                if runs_rows(i):
                    wait(dve, parts_done, i * 3 + 3 + 3 * LEAD)
                    nc.vector.tensor_tensor(diff_sq[:, :], half_diff[:, :], half_diff[:, :], ALU.mult).then_inc(diff_sq_done, 1)
                if edge_turn and not last_rows(i):
                    rows_to_write(m, um, 0, 2)
                if runs_rows(i):
                    wait(dve, diff_sq_done, i + 1 + LEAD)
                    nc.vector.scalar_tensor_tensor(out=var96[:, :], in0=diff_sq[:, :], scalar=D / 4.0, in1=sq_sum[:, :],
                                                   op0=ALU.mult, op1=ALU.add).then_inc(var_done, 1)
                if last_rows(i):
                    newton(i, u, None)
                    counts(m, om, um)
                    inverse_counts(m)
                    rows_to_write(m, um, 0, 2)
                if edge_turn:
                    rows_to_write(m, um, 2, TB)
                if ends(i, 0):
                    equality(j, oj, uj)
                if runs_step(j):
                    wait(dve, log1p_done, j + 1)
                    wait(dve, gate_done, j)
                    nc.vector.scalar_tensor_tensor(out=log_gate[:, :, :], in0=z_ps[uj % 2][:, :, 0:D], scalar=0.0,
                                                   in1=log1p[:, :, 0:D], op0=ALU.min, op1=ALU.subtract
                                                   ).then_inc(log_gate_done, 1)
                if runs_step(j):
                    wait(dve, message_done, j)
                    nc.vector.scalar_tensor_tensor(out=softplus[:, :, :], in0=z_ps[uj % 2][:, :, D:2 * D], scalar=0.0,
                                                   in1=log1p[:, :, D:2 * D], op0=ALU.max, op1=ALU.add
                                                   ).then_inc(softplus_done, 1)
                if ends(i, 0):
                    message(j)
                    counts(j, oj, uj)
                    inverse_counts(j)
                    rows_to_write(j, uj, 0, TB)
                if isinstance(i, int) and i in between_steps:
                    between_steps[i]()

            first_steps(step)
            steps(dve, step, 2, until=OUTER - 1)

            bad = dve.value_load(flag[0:1, 0:1], min_val=0, max_val=1)

            def tile_indices(t, n):
                dst_t = dst_col[:, bass.ds(t + 1, 1)]
                dve.wait_ge(r_written, n * 16 + 16)
                nc.vector.tensor_scalar(diag, ident[:, :], dst_t, None, ALU.mult).then_inc(r_diag_done, 1)
                dve.wait_ge(r_across_done, n + 1)
                nc.vector.tensor_scalar(r_same, r_ps[:, P:2 * P], dst_t, None, ALU.is_equal).then_inc(r_same_done, 1)
                dve.wait_ge(r_same_done, n + 1)
                nc.vector.tensor_tensor(r_later, r_same, later[:, :], ALU.mult).then_inc(r_later_done, 1)
                dve.wait_ge(r_sum_done, n + 1)
                nc.vector.tensor_scalar(r_mask[:, :], r_ps[:, D + 1:D + 2], 0.5, PAD, ALU.is_gt, ALU.mult).then_inc(r_mask_done, 1)
                nc.vector.tensor_scalar(r_gather_f[:, :], dst_t, float(NODES - 1), None, ALU.min).then_inc(r_mask_done, 1)
                dve.wait_ge(r_mask_done, n * 2 + 2)
                nc.vector.tensor_copy(r_gather[:, :], r_gather_f[:, :])
                nc.vector.tensor_tensor(r_scatter[:, :], r_mask[:, :], dst_t, ALU.add).then_inc(r_idx_done, 1)

            with dve.If(bad != 0):
                nc.vector.memset(zeros, 0.0).then_inc(r_zeroed, 1)
                with dve.Fori(0, TILES) as t:
                    tile_indices(t, t)
                    dve.wait_ge(r_gathered, t * 16 + 16)
                    nc.vector.tensor_tensor(r_count_new[:, :], r_count[:, :], r_ps[:, D:D + 1], ALU.add).then_inc(r_new_done, 1)
                with dve.Fori(0, TILES) as t:
                    tile_indices(t, t + TILES)
                    dve.wait_ge(r_gathered, t * 32 + 16 * TILES + 32)
                    nc.vector.tensor_scalar(r_count_new[:, :], r_count[:, :], 1.0, None, ALU.max).then_inc(r_clamped, 1)
                    dve.wait_ge(r_clamped, t + 1)
                    nc.vector.reciprocal(r_inv[:, :], r_count_new[:, :]).then_inc(r_inv_done, 1)
                    dve.wait_ge(r_inv_done, t + 1)
                    nc.vector.scalar_tensor_tensor(out=r_row_new[:, :], in0=r_ps[:, 0:D], scalar=r_inv[:, 0:1], in1=r_row[:, :],
                                                   op0=ALU.mult, op1=ALU.add).then_inc(r_new_done, 1)

        @block.tensor
        def _(pe):
            pe.wait_ge(const_done, 6)
            for n in range(3):
                pe.wait_ge(rows_f_done, n + 1)
                nc.tensor.transpose(cols_ps[n][:, 0:P], index_rows_f[:, n, 0, :], ident[:, :])
                k = TILES - P
                nc.tensor.transpose(cols_ps[n][:, P:TILES], index_rows_f[0:k, n, 1, :], ident[0:k, 0:k]).then_inc(cols_done, 1)
            pe.wait_ge(cols_read, 2)
            pe.wait_ge(message_ones_done, 1)
            pe.wait_ge(weights_loaded, 16 * 4)

            def sums(j):
                wait(pe, message_done, j + 1)
                wait(pe, same_done, j + 1)
                wait(pe, final_done, j)
                for t in range(TB):
                    if isinstance(j, int):
                        cur, prev = messages[:, j * TB + t, :], messages[:, max(j * TB + t - 1, 0), :]
                    else:
                        cur = messages[:, bass.ds(j * TB + t, 1), :].rearrange("p a c -> p (a c)")
                        prev = messages[:, bass.ds(j * TB + (t - 1), 1), :].rearrange("p a c -> p (a c)")
                    nc.tensor.matmul(sum_ps[:, t, :], same[:, 0, t, :], cur, start=True, stop=False)
                    last = nc.tensor.matmul(sum_ps[:, t, :], same[:, 1, t, :], prev, start=False, stop=True)
                last.then_inc(sum_done, 1)

            def step(i, o, u):
                if isinstance(i, int) and i == 2:
                    pe.wait_ge(violations_done, 1)
                    nc.tensor.matmul(r_ps[:, 0:1], ones[:, :], violations[:, :], start=True, stop=True
                                     ).then_inc(violations_summed, 1)
                k, ok, uk = back(i, o, u, 1)
                if runs_step(k):
                    wait(pe, edge_norm_done, k + 1)
                    pe.wait_ge(edge_loaded[uk], ok * 16 + (32 if isinstance(k, int) and k == STEPS - 1 else 16))
                    for h in range(2):
                        wait(pe, trans_out[h], k)
                        for t in range(2):
                            for b in range(2):
                                last = nc.tensor.transpose(trans_ps[h][:, t, b, :], concat[uk][:, 2 * h + t, b * P:(b + 1) * P],
                                                           ident[:, :])
                        last.then_inc(trans_done[h], 1)
                m = i - 3
                if runs_step(m) and not ends(i, 1):
                    sums(m)
                if runs_step(k):
                    wait(pe, softplus_done, k - 1)
                    for h in range(2):
                        wait(pe, trans_out[h], k + 1)
                        for t in range(2):
                            z = z_ps[uk % 2][:, 2 * h + t, 0:2 * D]
                            nc.tensor.matmul(z, ones[0:1, :], bias[0:1, :], start=True, stop=False)
                            for b in range(2):
                                last = nc.tensor.matmul(z, concat_t[:, h, t, b, :], weights[:, b, :], start=False, stop=(b == 1))
                    last.then_inc(z_done, 1)
                if ends(i, 0):
                    sums(i - 2)

            steps(pe, step, 2)

            pe.wait_ge(flag_done, 1)
            bad = pe.value_load(flag[0:1, 0:1], min_val=0, max_val=1)

            def tile_sums(t, n):
                pe.wait_ge(r_diag_done, n + 1)
                nc.tensor.matmul(r_ps[:, P:2 * P], ones[:, :], diag, start=True, stop=True).then_inc(r_across_done, 1)
                pe.wait_ge(r_later_done, n + 1)
                m = messages[:, bass.ds(t, 1), :].rearrange("p a c -> p (a c)")
                nc.tensor.matmul(r_ps[:, 0:D + 1], r_same, m, start=True, stop=True)
                nc.tensor.matmul(r_ps[:, D + 1:D + 2], r_later, ones[:, 0:1], start=True, stop=True).then_inc(r_sum_done, 1)

            with pe.If(bad != 0):
                with pe.Fori(0, TILES) as t:
                    tile_sums(t, t)
                with pe.Fori(0, TILES) as t:
                    tile_sums(t, t + TILES)


_INS = ["x", "src", "dst", "edge_attr_64", "L0_gnn_W_e", "L0_gnn_b_e", "L0_gnn_W_n", "L0_gnn_b_n"]


def kernel(**inputs):
    import numpy as _np
    import concourse.bacc as _bacc
    from concourse import mybir as _mybir
    from concourse.bass_utils import run_bass_kernel_spmd as _run

    nc = _bacc.Bacc("TRN2", target_bir_lowering=False, num_devices=1)
    arrays, args = {}, []
    for name in _INS:
        a = _np.ascontiguousarray(inputs[name])
        arrays[f"in_{name}"] = a
        args.append(nc.dram_tensor(f"in_{name}", a.shape, _mybir.dt.from_np(a.dtype), kind="ExternalInput").ap())
    out = nc.dram_tensor("out", (NODES, D), FP32, kind="ExternalOutput").ap()
    count_table = nc.dram_tensor("count_table", (NODES, 1), FP32, kind="Internal").ap()
    build(nc, *args, out, count_table)
    return _run(nc, [arrays], core_ids=[0]).results[0]["out"]
```
